# Optimizing a Trainium2 kernel written in Bass

```python
import numpy as np
import jax
import jax.numpy as jnp

def _softmax(x, axis=-1):
    return jax.nn.softmax(x, axis=axis)

def _gelu(x):
    return jax.nn.gelu(x, approximate=True)

def _silu(x):
    return jax.nn.silu(x)

def _sigmoid(x):
    return jax.nn.sigmoid(x)

def _layernorm(x, axis=-1, eps=1e-05):
    m = jnp.mean(x, axis=axis, keepdims=True)
    v = jnp.var(x, axis=axis, keepdims=True)
    return (x - m) / jnp.sqrt(v + eps)

def _scatter_add(tgt, idx, src, axis=0):
    return tgt.at[idx].add(src)

def _segment_sum(src, seg, n):
    return jax.ops.segment_sum(src, seg, n)
kernel_name = 'mk_seq_preln_d2_jaxref_r8_3f87ab'

def setup_inputs(seed: int=0):
    np.random.seed(seed)
    _w = jnp.asarray

    def _L0_attn_setup():
        import jax, jax.numpy as jnp
        import numpy as np
        EMBED = 128
        N_HEAD = 16
        HEAD_DIM = EMBED // N_HEAD
        key = jax.random.key(seed)
        ks = jax.random.split(key, 9)

        def xavier(k, shape, fan_in, fan_out):
            bound = float(np.sqrt(6.0 / (fan_in + fan_out)))
            return jax.random.uniform(k, shape, jnp.float32, -bound, bound)
        x = jax.random.normal(ks[0], (4, 256, EMBED), jnp.float32)
        wq = xavier(ks[1], (N_HEAD, EMBED, HEAD_DIM), EMBED, HEAD_DIM)
        wk = xavier(ks[2], (N_HEAD, EMBED, HEAD_DIM), EMBED, HEAD_DIM)
        wv = xavier(ks[3], (N_HEAD, EMBED, HEAD_DIM), EMBED, HEAD_DIM)
        bq = jnp.zeros((N_HEAD, 1, HEAD_DIM), jnp.float32)
        bk = jnp.zeros((N_HEAD, 1, HEAD_DIM), jnp.float32)
        bv = jnp.zeros((N_HEAD, 1, HEAD_DIM), jnp.float32)
        bnd = 1.0 / float(np.sqrt(EMBED))
        wo = jax.random.uniform(ks[4], (EMBED, EMBED), jnp.float32, -bnd, bnd)
        bo = jax.random.uniform(ks[5], (EMBED,), jnp.float32, -bnd, bnd)
        return {'x': x, 'wq': wq, 'bq': bq, 'wk': wk, 'bk': bk, 'wv': wv, 'bv': bv, 'wo': wo, 'bo': bo}
    _L0_attn_in = _L0_attn_setup()

    def _L0_ffn_setup():
        import jax, jax.numpy as jnp
        import numpy as np
        DIM = 128
        HIDDEN = 384
        SCALE = 1.0 / 127.0

        def _dequant(w_int, dtype):
            return w_int.astype(dtype) * jnp.asarray(SCALE, dtype)
        key = jax.random.key(seed)
        k_x, k_g, k_u, k_d = jax.random.split(key, 4)
        x = jax.random.normal(k_x, (4, 256, DIM), dtype=jnp.float32)
        w_gate = jax.random.randint(k_g, (HIDDEN, DIM), -127, 128, dtype=jnp.int32)
        w_up = jax.random.randint(k_u, (HIDDEN, DIM), -127, 128, dtype=jnp.int32)
        w_down = jax.random.randint(k_d, (DIM, HIDDEN), -127, 128, dtype=jnp.int32)
        return {'x': x, 'w_gate': w_gate, 'w_up': w_up, 'w_down': w_down}
    _L0_ffn_in = _L0_ffn_setup()

    def _L1_attn_setup():
        import jax, jax.numpy as jnp
        import numpy as np
        D = 128
        H = 16
        HD = D // H
        EPS = 1e-06

        def rms_norm(x, w):
            xf = x.astype(jnp.float32)
            rms = jnp.sqrt(jnp.mean(xf * xf, axis=-1, keepdims=True) + EPS)
            return (xf / rms * w.astype(jnp.float32)).astype(x.dtype)
        key = jax.random.key(seed)
        ks = jax.random.split(key, 6)
        B, S = (2, 256)
        x = jax.random.normal(ks[0], (B, S, D), dtype=jnp.float32)
        Wqkv = jax.random.normal(ks[1], (3 * D, D), dtype=jnp.float32) * (1.0 / np.sqrt(D))
        bqkv = jax.random.normal(ks[2], (3 * D,), dtype=jnp.float32) * 0.02
        Wproj = jax.random.normal(ks[3], (D, D), dtype=jnp.float32) * (1.0 / np.sqrt(D))
        bproj = jax.random.normal(ks[4], (D,), dtype=jnp.float32) * 0.02
        qn_w = jnp.ones((HD,), dtype=jnp.float32)
        kn_w = jnp.ones((HD,), dtype=jnp.float32)
        return {'x': x, 'Wqkv': Wqkv, 'bqkv': bqkv, 'Wproj': Wproj, 'bproj': bproj, 'qn_w': qn_w, 'kn_w': kn_w}
    _L1_attn_in = _L1_attn_setup()

    def _L1_ffn_setup():
        import jax, jax.numpy as jnp
        import numpy as np
        B, S, IN, OUT, E, R = (8, 512, 128, 128, 8, 8)
        LORA_ALPHA = 16
        SCALING = LORA_ALPHA / R
        key = jax.random.key(seed)
        k = jax.random.split(key, 6)
        x = jax.random.normal(k[0], (B, S, IN), dtype=jnp.float32)
        base_w = jax.random.normal(k[1], (OUT, IN), dtype=jnp.float32) * 0.02
        base_b = jnp.zeros((OUT,), dtype=jnp.float32)
        lora_A = jax.random.normal(k[2], (IN, R), dtype=jnp.float32) * 0.02
        lora_B = jax.random.normal(k[3], (E, R, OUT), dtype=jnp.float32) * 0.02
        router_w = jax.random.normal(k[4], (E, IN), dtype=jnp.float32) * 0.02
        router_b = jnp.zeros((E,), dtype=jnp.float32)
        return {'x': x, 'base_w': base_w, 'base_b': base_b, 'lora_A': lora_A, 'lora_B': lora_B, 'router_w': router_w, 'router_b': router_b}
    _L1_ffn_in = _L1_ffn_setup()
    _d = {'L0_attn_x': _L0_attn_in['x'], 'L0_attn_wq': _L0_attn_in['wq'], 'L0_attn_bq': _L0_attn_in['bq'], 'L0_attn_wk': _L0_attn_in['wk'], 'L0_attn_bk': _L0_attn_in['bk'], 'L0_attn_wv': _L0_attn_in['wv'], 'L0_attn_bv': _L0_attn_in['bv'], 'L0_attn_wo': _L0_attn_in['wo'], 'L0_attn_bo': _L0_attn_in['bo'], 'L0_ffn_w_gate': _L0_ffn_in['w_gate'], 'L0_ffn_w_up': _L0_ffn_in['w_up'], 'L0_ffn_w_down': _L0_ffn_in['w_down'], 'L1_attn_Wqkv': _L1_attn_in['Wqkv'], 'L1_attn_bqkv': _L1_attn_in['bqkv'], 'L1_attn_Wproj': _L1_attn_in['Wproj'], 'L1_attn_bproj': _L1_attn_in['bproj'], 'L1_attn_qn_w': _L1_attn_in['qn_w'], 'L1_attn_kn_w': _L1_attn_in['kn_w'], 'L1_ffn_base_w': _L1_ffn_in['base_w'], 'L1_ffn_base_b': _L1_ffn_in['base_b'], 'L1_ffn_lora_A': _L1_ffn_in['lora_A'], 'L1_ffn_lora_B': _L1_ffn_in['lora_B'], 'L1_ffn_router_w': _L1_ffn_in['router_w'], 'L1_ffn_router_b': _L1_ffn_in['router_b']}
    _x0 = _d['L0_attn_x']
    _d['L0_attn_x'] = jax.random.normal(jax.random.fold_in(jax.random.key(seed), 1), (16, 512, 128), dtype=_x0.dtype)
    del _x0
    return _d

def reference(L0_attn_x, L0_attn_wq, L0_attn_bq, L0_attn_wk, L0_attn_bk, L0_attn_wv, L0_attn_bv, L0_attn_wo, L0_attn_bo, L0_ffn_w_gate, L0_ffn_w_up, L0_ffn_w_down, L1_attn_Wqkv, L1_attn_bqkv, L1_attn_Wproj, L1_attn_bproj, L1_attn_qn_w, L1_attn_kn_w, L1_ffn_base_w, L1_ffn_base_b, L1_ffn_lora_A, L1_ffn_lora_B, L1_ffn_router_w, L1_ffn_router_b):

    def _L0_attn_ref(x, wq, bq, wk, bk, wv, bv, wo, bo):
        import jax, jax.numpy as jnp
        import numpy as np
        EMBED = 128
        N_HEAD = 16
        HEAD_DIM = EMBED // N_HEAD
        q = jnp.einsum('bsd,hde->bhse', x, wq) + bq
        k = jnp.einsum('bsd,hde->bhse', x, wk) + bk
        v = jnp.einsum('bsd,hde->bhse', x, wv) + bv
        scale = 1.0 / jnp.sqrt(jnp.asarray(q.shape[-1], q.dtype))
        scores = jax.nn.softmax(jnp.einsum('bhse,bhte->bhst', q, k) * scale, axis=-1)
        att = jnp.einsum('bhst,bhte->bhse', scores, v)
        b, h, s, e = att.shape
        att = att.transpose(0, 2, 1, 3).reshape(b, s, h * e)
        return att @ wo.T + bo

    def _L0_ffn_ref(x, w_gate, w_up, w_down):
        import jax, jax.numpy as jnp
        import numpy as np
        DIM = 128
        HIDDEN = 384
        SCALE = 1.0 / 127.0

        def _dequant(w_int, dtype):
            return w_int.astype(dtype) * jnp.asarray(SCALE, dtype)
        wg = _dequant(w_gate, x.dtype)
        wu = _dequant(w_up, x.dtype)
        wd = _dequant(w_down, x.dtype)
        gate = jnp.einsum('bsd,hd->bsh', x, wg)
        up = jnp.einsum('bsd,hd->bsh', x, wu)
        h = jax.nn.silu(gate) * up
        return jnp.einsum('bsh,dh->bsd', h, wd)

    def _L1_attn_ref(x, Wqkv, bqkv, Wproj, bproj, qn_w, kn_w):
        import jax, jax.numpy as jnp
        import numpy as np
        D = 128
        H = 16
        HD = D // H
        EPS = 1e-06

        def rms_norm(x, w):
            xf = x.astype(jnp.float32)
            rms = jnp.sqrt(jnp.mean(xf * xf, axis=-1, keepdims=True) + EPS)
            return (xf / rms * w.astype(jnp.float32)).astype(x.dtype)
        B, S, _ = x.shape
        qkv = x @ Wqkv.T + bqkv
        qkv = qkv.reshape(B, S, 3, H, HD)
        q, k, v = (qkv[:, :, 0], qkv[:, :, 1], qkv[:, :, 2])
        q = rms_norm(q, qn_w)
        k = rms_norm(k, kn_w)
        q = q.transpose(0, 2, 1, 3)
        k = k.transpose(0, 2, 1, 3)
        v = v.transpose(0, 2, 1, 3)
        scale = 1.0 / np.sqrt(HD)
        scores = jnp.einsum('bhsd,bhtd->bhst', q, k) * scale
        attn = jax.nn.softmax(scores, axis=-1)
        out = jnp.einsum('bhst,bhtd->bhsd', attn, v)
        out = out.transpose(0, 2, 1, 3).reshape(B, S, D)
        return out @ Wproj.T + bproj

    def _L1_ffn_ref(x, base_w, base_b, lora_A, lora_B, router_w, router_b):
        import jax, jax.numpy as jnp
        import numpy as np
        B, S, IN, OUT, E, R = (8, 512, 128, 128, 8, 8)
        LORA_ALPHA = 16
        SCALING = LORA_ALPHA / R
        result = jnp.einsum('bsd,od->bso', x, base_w) + base_b
        logits = jnp.einsum('bsd,ed->bse', x, router_w) + router_b
        gating = jax.nn.softmax(logits, axis=-1).astype(jnp.bfloat16)
        mid = jnp.einsum('bsd,dr->bsr', x, lora_A)
        lora_out = jnp.einsum('bsr,erd,bse->bsd', mid, lora_B, gating.astype(jnp.float32))
        return result + lora_out * SCALING
    x = L0_attn_x
    x = x + _L0_attn_ref(_layernorm(x, axis=-1), L0_attn_wq, L0_attn_bq, L0_attn_wk, L0_attn_bk, L0_attn_wv, L0_attn_bv, L0_attn_wo, L0_attn_bo)
    x = x + _L0_ffn_ref(_layernorm(x, axis=-1), L0_ffn_w_gate, L0_ffn_w_up, L0_ffn_w_down)
    x = x + _L1_attn_ref(_layernorm(x, axis=-1), L1_attn_Wqkv, L1_attn_bqkv, L1_attn_Wproj, L1_attn_bproj, L1_attn_qn_w, L1_attn_kn_w)
    x = x + _L1_ffn_ref(_layernorm(x, axis=-1), L1_ffn_base_w, L1_ffn_base_b, L1_ffn_lora_A, L1_ffn_lora_B, L1_ffn_router_w, L1_ffn_router_b)
    return x

_drawn_inputs = setup_inputs


def setup_inputs(seed=0):
    import zlib

    import numpy as np

    out = dict(_drawn_inputs(seed))
    spreads = {'L0_attn_bq': (0.0, 0.338),
     'L0_attn_bk': (0.0, 2.0),
     'L0_attn_bv': (0.0, 0.1),
     'L1_attn_qn_w': (1.0, 0.6),
     'L1_attn_kn_w': (1.0, 0.6),
     'L1_ffn_base_b': (0.0, 2.0),
     'L1_ffn_router_b': (0.0, 2.0)}
    factors = {'L1_attn_Wqkv': 8.0,
     'L1_attn_bqkv': 64.0,
     'L1_attn_Wproj': 8.0,
     'L1_attn_bproj': 200.0,
     'L1_ffn_base_w': 64.0,
     'L1_ffn_lora_A': 64.0,
     'L1_ffn_lora_B': 64.0,
     'L1_ffn_router_w': 64.0}
    for name, (base, spread) in spreads.items():
        noise = np.random.default_rng([zlib.crc32(name.encode()), seed]).standard_normal(out[name].shape)
        drawn = base * np.exp(spread * noise) if base else spread * noise
        out[name] = jnp.asarray(drawn.astype(out[name].dtype))
    for name, factor in factors.items():
        out[name] = (out[name] * factor).astype(out[name].dtype)
    return out
```

```python
import numpy as np
import concourse.bass as bass
from concourse import mybir
from contextlib import ExitStack

F32 = mybir.dt.float32
BF16 = mybir.dt.bfloat16
I32 = mybir.dt.int32
ALU = mybir.AluOpType
ACT = mybir.ActivationFunctionType
AX = mybir.AxisListType

BATCH, SEQ, D = 16, 512, 128
HEADS, HD = 16, 8
HID = 384
TT = SEQ // 128
NH = HID // 128
EXPERTS, RANK = 8, 8
LORA_SCALE = 2.0
DEQUANT = float(np.float32(1.0 / 127.0))
QK_SCALE = float(1.0 / np.sqrt(HD))
LN_EPS, RMS_EPS = 1e-5, 1e-6

PAIRS = HEADS // 2
PARTS = 3
TERMS = 6
Q_PART = (0, 0, 0, 1, 1, 2)
K_PART = (0, 1, 2, 0, 1, 0)
KROWS = HD * TERMS
MROWS = 2
QROWS = 2 * KROWS

STEPS = 32
LEAD = 12
RING = 8

X_PE = ((4, "qt"), (6, "kt"), (8, "v1"), (9, "xt0"), (11, "q0"), (12, "m0b"), (13, "pr1"), (15, "k0"),
        (17, "xt3"), (19, "rt"), (23, "ct"), (25, "out"), (28, "m1a"))
Y_PE = ((6, "v0"), (12, "m1b"), (13, "pr0"), (17, "xt1"), (18, "g0"), (19, "u0"), (20, "g1"), (21, "u1"),
        (22, "g2"), (23, "u2"), (24, "dn"), (28, "m0a"), (29, "xt2"), (30, "qka"), (31, "qkb"))
PIECE = {"qt": (-1, "M2"), "kt": (-1, "M2"), "v1": (-1, "M2"), "xt0": (1, "P0"), "q0": (1, "P0"), "k0": (1, "P0"),
         "m0b": (0, "MXt"), "pr1": (-2, "E"), "xt3": (-2, "E"), "rt": (-2, "E"), "ct": (-2, "E"), "out": (-2, "E"),
         "m1a": (-1, "MXh"),
         "v0": (1, "V0"), "m1b": (-1, "MXt"), "m0a": (1, "MXh"), "pr0": (0, "M1"), "xt1": (0, "M1"),
         "g0": (0, "M1"), "u0": (0, "M1"), "g1": (0, "M1"), "u1": (0, "M1"), "g2": (0, "M1"), "u2": (0, "M1"),
         "dn": (0, "M1"), "xt2": (0, "M1"), "qka": (0, "M1"), "qkb": (0, "M1")}


def parts_of(kind, i):
    if kind == "X":
        have = (("A", i < BATCH), ("At", 1 <= i - 1 + 0 and i - 2 >= 0), ("MXt", i < BATCH),
                ("MXh", 1 <= i <= BATCH), ("M2", 1 <= i <= BATCH), ("P0", i + 1 < BATCH), ("E", i >= 2))
    else:
        have = (("A", 1 <= i <= BATCH), ("At", 0 <= i < BATCH), ("MXt", 1 <= i <= BATCH),
                ("MXh", i + 1 < BATCH), ("M1", 0 <= i < BATCH), ("V0", i + 1 < BATCH))
    return frozenset(n for n, yes in have if yes)


def slot_pieces(kind, i):
    have = parts_of(kind, i)
    return [(s, n) for s, n in (X_PE if kind == "X" else Y_PE) if PIECE[n][1] in have]


SLOTS = [("Y", -1)] + [(k, i) for i in range(BATCH + 2) for k in "XY" if (k, i) != ("Y", BATCH + 1)]
LOOP_FROM, LOOP_TO = 2, BATCH - 1
assert all(parts_of("X", i) == parts_of("X", 2) and parts_of("Y", i - 1) == parts_of("Y", 2)
           for i in range(LOOP_FROM, LOOP_TO))


def piece_before(kind, i, name):
    seen = []
    for k, j in SLOTS:
        for _, n in slot_pieces(k, j):
            if (k, j, n) == (kind, i, name):
                return (seen[-1][0], seen[-1][1] - i) if seen else None
            seen.append((n, j + PIECE[n][0]))
            if k == "Y" and j == -1 and n == "v0":
                pass
    raise AssertionError(name)


def attends_before(layer, b):
    if isinstance(b, int):
        return (max(2 * b - 1, 0) if layer == 0 else min(2 * b + 2, 2 * BATCH - 1))
    return 2 * b - 1 if layer == 0 else 2 * b + 2


def maxima_before(layer, b):
    return attends_before(layer, b)


def wide(ap, dim, n):
    shape = list(ap.shape)
    shape[dim] = n
    return ap.broadcast_to(shape)


def need(eng, sem, value):
    if isinstance(value, int) and value <= 0:
        return
    eng.wait_ge(sem, value)


def wait_apart(eng, sem, value, passed):
    need(eng, sem, value)
    if not isinstance(value, int):
        eng.sem_inc(passed, 1)


def build(nc, T, out_dram):
    ctx = ExitStack()
    with ctx:
        def sb(name, shape, dt=F32):
            return ctx.enter_context(nc.sbuf_tensor(name, shape, dt))

        def sem(name):
            return ctx.enter_context(nc.semaphore(name))

        q_rows = [nc.dram_tensor(f"q_rows{l}", (128, TERMS, SEQ), BF16).ap() for l in (0, 1)]
        k_rows = [nc.dram_tensor(f"k_rows{l}", (128, TERMS, SEQ), BF16).ap() for l in (0, 1)]
        rden_rows = [nc.dram_tensor(f"rden_rows{l}", (8, 2 * SEQ), F32).ap() for l in (0, 1)]

        ident = sb("ident", [128, 128])
        wq = sb("wq", [128, D])
        wk = sb("wk", [128, D])
        wv = sb("wv", [128, D])
        qk_bias = sb("qk_bias", [128, 2])
        bq_scaled = sb("bq_scaled", [128, 1])
        v_bias = [sb(f"v_bias{l}", [128, D]) for l in (0, 1)]
        wo = [sb(f"wo{l}", [128, 2, D]) for l in (0, 1)]
        w_gate = sb("w_gate", [128, NH, 128])
        w_up = sb("w_up", [128, NH, 128])
        w_down = sb("w_down", [128, NH, D])
        wqkv = sb("wqkv", [128, 3 * D])
        qk1_bias = sb("qk1_bias", [128, 2 * D])
        norm_w = sb("norm_w", [128, 2])
        qn_scaled = sb("qn_scaled", [128, 1])
        w_base = sb("w_base", [128, D])
        w_mid = sb("w_mid", [128, 2 * EXPERTS])
        mid_bias = sb("mid_bias", [128, 2 * EXPERTS])
        w_lora = sb("w_lora", [EXPERTS * RANK + 1, D])
        half_neg = sb("half_neg", [128, TT])

        x_in = sb("x_in", [128, TT, D])
        res = [sb(f"res{l}", [128, TT, D]) for l in (0, 1)]
        x1 = sb("x1", [128, TT, D])
        x2 = sb("x2", [128, TT, D])
        x3 = sb("x3", [128, TT, D])
        bn = [sb(f"bn{k}", [128, TT, 6]) for k in range(4)]
        mv = [sb(f"mv{k}", [128, TT, 2]) for k in range(4)]
        vpe = [sb(f"vpe{k}", [128, TT]) for k in range(4)]
        rstd = [sb(f"rstd{k}", [128, TT]) for k in range(4)]
        xn = [sb(f"xn{k}", [128, TT, D]) for k in (0, 1, 3)]
        xn.insert(2, xn[1])
        xnt = [sb(f"xnt{k}", [128, SEQ]) for k in range(4)]

        qf = [[sb(f"{c}f{l}", [128, SEQ]) for c in "qk"] for l in (0, 1)]
        qp = [[sb(f"{c}p{l}", [128, PARTS, SEQ], BF16) for c in "qk"] for l in (0, 1)]
        q_stack = [sb(f"q_stack{l}", [128, PAIRS, SEQ], BF16) for l in (0, 1)]
        k_stack = [[sb(f"k_stack{l}{e}", [128, PAIRS, SEQ], BF16) for e in (0, 1)] for l in (0, 1)]
        v_aug = [sb(f"v_aug{l}", [128, TT, HEADS, 32]) for l in (0, 1)]
        neg_max = [sb(f"neg_max{l}", [128, 2, TT, 8]) for l in (0, 1)]
        m_parts = [[sb(f"m_parts{l}{h}", [8, MROWS, SEQ], BF16) for h in (0, 1)] for l in (0, 1)]
        probs = sb("probs", [128, RING, 2, SEQ])
        o_raw = [sb(f"o_raw{l}", [128, 2, SEQ]) for l in (0, 1)]
        rden_all = [sb(f"rden_all{l}", [128, 2, SEQ]) for l in (0, 1)]
        den = [sb(f"den{l}", [128, 64]) for l in (0, 1)]
        rden = [sb(f"rden{l}", [128, 64]) for l in (0, 1)]

        th = sb("th", [128, SEQ])
        gs = sb("gs", [128, SEQ])
        ht = sb("ht", [128, NH, SEQ])
        qk1 = sb("qk1", [128, TT, 2 * D])
        sq = ht[:, 0:2, :].rearrange("p c (t n) -> p (c t) n", n=2 * D)
        ms = sb("ms", [128, TT * 32])
        nw_y = sb("nw_y", [128, TT * 32])
        nw_t = sb("nw_t", [128, TT * 32])
        nw_u = sb("nw_u", [128, TT * 32])

        rm = sb("rm", [128, TT, 2 * EXPERTS])
        lmax = sb("lmax", [128, TT])
        lsh = sb("lsh", [128, TT, EXPERTS])
        lexp = sb("lexp", [128, TT, EXPERTS])
        lsum = sb("lsum", [128, TT])
        lrec = sb("lrec", [128, TT])
        gating = sb("gating", [128, TT, EXPERTS], BF16)
        coef = sb("coef", [128, TT, EXPERTS * RANK])
        coef_t = sb("coef_t", [EXPERTS * RANK + 1, SEQ])

        stage = probs[:, :, :, :].rearrange("p a b c -> p (a b c)")
        wo_nat = [stage[:, l * 128:(l + 1) * 128] for l in (0, 1)]
        wo_perm = [stage[:, 256 + l * 256:512 + l * 256] for l in (0, 1)]
        bo_col = [stage[:, 768 + l:769 + l] for l in (0, 1)]
        int_w = [stage[:, 1024 + 384 * n:1408 + 384 * n].bitcast(I32) for n in range(3)]
        flt_w = [stage[:, 2304 + 384 * n:2688 + 384 * n] for n in range(3)]
        wqkv_nat = stage[:, 3584:3968]
        base_nat = stage[:, 3968:4096]
        router_nat = stage[0:EXPERTS, 4096:4224]
        lora_nat = stage[0:EXPERTS * RANK, 4224:4352]

        ps = ctx.enter_context(nc.psum_tensor("ps", [128, 8, 512], F32))
        acc = ps[:, 6, :]
        gen = ps[:, 7, :]
        gen4 = gen.rearrange("p (t n) -> p t n", t=TT)

        w_loaded = sem("w_loaded")
        k_zeros = sem("k_zeros")
        k_both = sem("k_both")
        k_ones = sem("k_ones")
        v_zeros = sem("v_zeros")
        ident_zero = sem("ident_zero")
        ident_ready = sem("ident_ready")
        w_placed = sem("w_placed")
        w_turned = sem("w_turned")
        w_ready = sem("w_ready")
        written = {n: sem(f"{n}_written") for n in PIECE}
        read = {n: sem(f"{n}_read") for n in PIECE}
        x_loaded = sem("x_loaded")
        res_copied = [sem(f"res_copied{l}") for l in (0, 1)]
        bn_done = [sem(f"bn_done{k}") for k in range(4)]
        mv_done = [sem(f"mv_done{k}") for k in range(4)]
        var_ready = [sem(f"var_ready{k}") for k in range(4)]
        rstd_ready = [sem(f"rstd_ready{k}") for k in range(4)]
        xn_ready = [sem(f"xn_ready{k}") for k in range(4)]
        resid1 = [sem(f"{c}_resid1") for c in ("q0", "k0", "q1", "k1")]
        part1 = [sem(f"{c}_part1") for c in ("q0", "k0", "q1", "k1")]
        part2 = [sem(f"{c}_part2") for c in ("q0", "k0", "q1", "k1")]
        rows_out = [[sem(f"{c}rows_out{l}") for c in "qk"] for l in (0, 1)]
        stack_in = [[sem(f"stack_in{l}{h}") for h in (0, 1)] for l in (0, 1)]
        m_part0 = [[sem(f"m_part0_{l}{h}") for h in (0, 1)] for l in (0, 1)]
        m_in = [[sem(f"m_in{l}{h}") for h in (0, 1)] for l in (0, 1)]
        v_half = [sem(f"v_half{l}") for l in (0, 1)]
        max_scores = sem("max_scores")
        max_taken = sem("max_taken")
        scores = sem("scores")
        exps = sem("exps")
        pv = sem("pv")
        o_saved = sem("o_saved")
        den_in = [sem(f"den_in{l}") for l in (0, 1)]
        rden_ready = [sem(f"rden_ready{l}") for l in (0, 1)]
        rden_out = [sem(f"rden_out{l}") for l in (0, 1)]
        rden_in = [sem(f"rden_in{l}") for l in (0, 1)]
        att_ready = [sem(f"att_ready{l}") for l in (0, 1)]
        tanh_done = sem("tanh_done")
        squared = sem("squared")
        newton = sem("newton")
        qk_normed = sem("qk_normed")
        moe = sem("moe")
        l_exp = sem("l_exp")
        m_rec = sem("m_rec")
        gate_ready = sem("gate_ready")
        coef_ready = sem("coef_ready")
        stored = sem("stored")
        passed = sem("passed")
        N_NEWTON = 13

        block = ctx.enter_context(nc.Block())

        def walk(eng, slot):
            for k, i in SLOTS:
                if LOOP_FROM <= i < LOOP_TO:
                    if (k, i) == ("X", LOOP_FROM):
                        with eng.Fori(LOOP_FROM, LOOP_TO) as it:
                            slot("X", it, LOOP_FROM)
                            slot("Y", it, LOOP_FROM)
                else:
                    slot(k, i, i)

        @block.sync
        def _(sp):
            def hold(sem, value):
                wait_apart(sp, sem, value, passed)

            def load(dst, src):
                sp.dma_start(dst, src).then_inc(w_loaded, 16)

            sp.dma_start(x_in[:, :, :], T["L0_attn_x"][0].rearrange("(t p) d -> p t d", p=128)).then_inc(x_loaded, 16)
            load(wq[:, :].rearrange("d (h e) -> d h e", h=HEADS), T["L0_attn_wq"].rearrange("h d e -> d h e"))
            load(wk[:, :].rearrange("d (h e) -> d h e", h=HEADS), T["L0_attn_wk"].rearrange("h d e -> d h e"))
            load(wv[:, :].rearrange("d (h e) -> d h e", h=HEADS), T["L0_attn_wv"].rearrange("h d e -> d h e"))
            load(qk_bias[:, 0:1], bass.AP(T["L0_attn_bq"].tensor, 0, [[1, 128], [1, 1]]))
            load(qk_bias[:, 1:2], bass.AP(T["L0_attn_bk"].tensor, 0, [[1, 128], [1, 1]]))
            load(v_bias[0][:, :], bass.AP(T["L0_attn_bv"].tensor, 0, [[0, 128], [1, 128]]))
            load(wo_nat[0], T["L0_attn_wo"])
            load(wo_nat[1], T["L1_attn_Wproj"])
            load(bo_col[0], bass.AP(T["L0_attn_bo"].tensor, 0, [[1, 128], [1, 1]]))
            load(bo_col[1], bass.AP(T["L1_attn_bproj"].tensor, 0, [[1, 128], [1, 1]]))
            load(int_w[0].rearrange("p (c f) -> p c f", c=NH), T["L0_ffn_w_gate"].rearrange("(c p) f -> p c f", p=128))
            load(int_w[1].rearrange("p (c f) -> p c f", c=NH), T["L0_ffn_w_up"].rearrange("(c p) f -> p c f", p=128))
            load(int_w[2], T["L0_ffn_w_down"])
            load(wqkv_nat.rearrange("p (c f) -> p c f", c=3), T["L1_attn_Wqkv"].rearrange("(c p) f -> p c f", p=128))
            load(qk1_bias[:, :], bass.AP(T["L1_attn_bqkv"].tensor, 0, [[0, 128], [1, 256]]))
            load(v_bias[1][:, :], bass.AP(T["L1_attn_bqkv"].tensor, 256, [[0, 128], [1, 128]]))
            load(norm_w[:, 0:1], bass.AP(T["L1_attn_qn_w"].tensor, 0, [[0, HEADS], [1, HD], [1, 1]]))
            load(norm_w[:, 1:2], bass.AP(T["L1_attn_kn_w"].tensor, 0, [[0, HEADS], [1, HD], [1, 1]]))
            load(base_nat, T["L1_ffn_base_w"])
            load(router_nat, T["L1_ffn_router_w"])
            load(w_mid[:, EXPERTS:], T["L1_ffn_lora_A"])
            load(lora_nat, T["L1_ffn_lora_B"].rearrange("e r d -> (e r) d"))
            load(w_lora[64:65, :], bass.AP(T["L1_ffn_base_b"].tensor, 0, [[0, 1], [1, 128]]))
            load(mid_bias[:, 0:EXPERTS], bass.AP(T["L1_ffn_router_b"].tensor, 0, [[0, 128], [1, 8]]))
            hold(x_loaded, 16)
            sp.dma_start(res[0][:, :, :], x_in[:, :, :]).then_inc(res_copied[0], 16)

            def load_x(b):
                hold(xn_ready[0], b)
                hold(res_copied[0], 16 * b)
                src = T["L0_attn_x"][bass.ds(b, 1)] if not isinstance(b, int) else T["L0_attn_x"][b:b + 1]
                sp.dma_start(x_in[:, :, :], src.rearrange("a (t p) d -> p (a t) d", p=128)).then_inc(x_loaded, 16)

            def parts_out(l, b):
                for n, (rows, pick) in enumerate(((q_rows[l], Q_PART), (k_rows[l], K_PART))):
                    for h in (0, 1):
                        hold(stack_in[l][h], 64 * b)
                    hold(part2[2 * l + n], b + 1)
                    for j0, j1 in ((0, 3), (3, 5), (5, 6)):
                        step = pick[j0 + 1] - pick[j0] if j1 - j0 > 1 else 0
                        sp.dma_start(rows[:, j0:j1, :],
                                     bass.AP(qp[l][n][:, :, :].tensor, pick[j0] * SEQ,
                                             [[PARTS * SEQ, 128], [step * SEQ, j1 - j0], [1, SEQ]])
                                     ).then_inc(rows_out[l][n], 16)

            def stack_half(l, half, b):
                for n in (0, 1):
                    hold(rows_out[l][n], 48 * (b + 1))
                if not isinstance(b, int) or b > 0:
                    hold(scores, STEPS * attends_before(l, b - 1) + 16 * (half + 1))
                for rows, stacks in ((q_rows[l], (q_stack[l], q_stack[l])), (k_rows[l], k_stack[l])):
                    for e in (0, 1):
                        src = bass.AP(rows.tensor, (64 * e + 32 * half) * TERMS * SEQ,
                                      [[SEQ, KROWS], [HD * TERMS * SEQ, 4], [1, SEQ]])
                        sp.dma_start(stacks[e][KROWS * e:KROWS * e + KROWS, 4 * half:4 * half + 4, :], src
                                     ).then_inc(stack_in[l][half], 16)

            def max_rows(l, half, b):
                hold(read[f"m{l}{'ab'[half]}"], b + 1)
                for e in (0, 1):
                    for j in range(MROWS):
                        row = QROWS + MROWS * e + j
                        sp.dma_start(q_stack[l][row:row + 1, 4 * half:4 * half + 4, :],
                                     m_parts[l][half][4 * e:4 * e + 4, j, :]).then_inc(m_in[l][half], 16)

            def den_lines(l, b):
                hold(o_saved, 2 * attends_before(l, b) + 2)
                sp.dma_start(den[l][:, :],
                             bass.AP(o_raw[l][:, :, :].tensor, 8 * 2 * SEQ, [[16 * 2 * SEQ, 8], [64, 16], [1, 64]])
                             ).then_inc(den_in[l], 16)

            def rden_lines(l, b):
                hold(rden_ready[l], b + 1)
                hold(rden_in[l], 16 * b)
                sp.dma_start(bass.AP(rden_rows[l].tensor, 0, [[64, 128], [1, 64]]), rden[l][:, :]
                             ).then_inc(rden_out[l], 16)
                hold(rden_out[l], 16 * (b + 1))
                hold(att_ready[l], b)
                sp.dma_start(rden_all[l][:, :, :].rearrange("p c s -> p (c s)"),
                             bass.AP(rden_rows[l].tensor, 0, [[2 * SEQ, 8], [0, 16], [1, 2 * SEQ]])
                             ).then_inc(rden_in[l], 16)

            def slot(kind, i, at):
                have = parts_of(kind, at)
                if kind == "X":
                    if "P0" in have:
                        load_x(i + 1)
                    if "E" in have:
                        den_lines(1, i - 2)
                    if "M2" in have:
                        parts_out(1, i - 1)
                    if "E" in have:
                        rden_lines(1, i - 2)
                    if "M2" in have:
                        stack_half(1, 0, i - 1)
                        stack_half(1, 1, i - 1)
                    if "MXt" in have:
                        max_rows(0, 1, i)
                    if "P0" in have:
                        parts_out(0, i + 1)
                    if "M2" in have:
                        hold(read["dn"], i)
                        if "E" in have:
                            hold(read["pr1"], i - 1)
                        sp.dma_start(res[1][:, :, :], x2[:, :, :]).then_inc(res_copied[1], 16)
                    if "P0" in have:
                        stack_half(0, 0, i + 1)
                    if "E" in have:
                        hold(read["out"], i - 1)
                        dst = out_dram[at - 2:at - 1] if isinstance(i, int) else out_dram[bass.ds(i - 2, 1)]
                        sp.dma_start(dst.rearrange("a (t p) d -> p (a t) d", p=128), x3[:, :, :]).then_inc(stored, 16)
                    if "MXh" in have:
                        max_rows(1, 0, i - 1)
                    if "P0" in have:
                        stack_half(0, 1, i + 1)
                else:
                    if at == -1:
                        parts_out(0, 0)
                        hold(k_ones, 4)
                        stack_half(0, 0, 0)
                        stack_half(0, 1, 0)
                        max_rows(0, 0, 0)
                        return
                    if "M1" in have:
                        den_lines(0, i)
                        rden_lines(0, i)
                    if "MXt" in have:
                        max_rows(1, 1, i - 1)
                    if "V0" in have:
                        hold(read["pr0"], i + 1)
                        hold(x_loaded, 16 * (i + 2))
                        sp.dma_start(res[0][:, :, :], x_in[:, :, :]).then_inc(res_copied[0], 16)
                    if "MXh" in have:
                        max_rows(0, 0, i + 1)

            walk(sp, slot)
            hold(stored, 16 * BATCH)

        @block.gpsimd
        def _(pool):
            pool.memset(ident[:, :], 0.0).then_inc(ident_zero, 1)
            pool.wait_ge(ident_zero, 1)
            pool.affine_select(out=ident[:, :], in_=ident[:, :], compare_op=ALU.not_equal, fill=1.0, base=0,
                               pattern=[[-1, 128]], channel_multiplier=1).then_inc(ident_ready, 1)
            pool.memset(half_neg[:, :], -0.5)
            pool.memset(mid_bias[:, EXPERTS:], 0.0)
            flat = [t[:, :, :].rearrange("p a b -> p (a b)") for t in (*k_stack[0], *k_stack[1], *q_stack)]
            for t in flat:
                pool.memset(t.bitcast(F32), 0.0).then_inc(k_zeros, 1)

            def apply_norm(k, x, b):
                pool.wait_ge(var_ready[k], b + 1)
                pool.tensor_tensor(rstd[k][:, :], vpe[k][:, :], half_neg[:, :], ALU.pow).then_inc(rstd_ready[k], 1)
                pool.wait_ge(rstd_ready[k], b + 1)
                wait_apart(pool, read[f"xt{k}"], b, passed)
                for t in range(TT):
                    last = pool.tensor_scalar(xn[k][:, t, :], x[:, t, :], mv[k][:, t, 0:1], rstd[k][:, t:t + 1],
                                              ALU.subtract, ALU.mult)
                last.then_inc(xn_ready[k], 1)

            def residual1(l, n, b):
                pool.wait_ge(read[(("q0", "k0"), ("qt", "kt"))[l][n]], b + 1)
                pool.tensor_tensor(qf[l][n][:, :], qf[l][n][:, :], qp[l][n][:, 0, :], ALU.subtract
                                   ).then_inc(resid1[2 * l + n], 1)

            def residual2(l, n, b):
                pool.wait_ge(part1[2 * l + n], b + 1)
                pool.tensor_tensor(qp[l][n][:, 2, :], qf[l][n][:, :], qp[l][n][:, 1, :], ALU.subtract
                                   ).then_inc(part2[2 * l + n], 1)

            def normalise(l, b):
                pool.wait_ge(rden_in[l], 16 * (b + 1))
                pool.tensor_tensor(o_raw[l][:, :, :], o_raw[l][:, :, :], rden_all[l][:, :, :], ALU.mult
                                   ).then_inc(att_ready[l], 1)

            def square(b):
                pool.wait_ge(read["qkb"], b + 1)
                pool.tensor_tensor(sq[:, :, :], qk1[:, :, :], qk1[:, :, :], ALU.mult).then_inc(squared, 1)

            def scale_qk(b):
                pool.wait_ge(newton, N_NEWTON * (b + 1))
                pool.tensor_tensor(qk1[:, :, :].rearrange("p t (g e) -> p (t g) e", e=HD),
                                   qk1[:, :, :].rearrange("p t (g e) -> p (t g) e", e=HD),
                                   wide(nw_y[:, :, None], 2, HD), ALU.mult).then_inc(qk_normed, 1)

            def mix(b):
                pool.wait_ge(gate_ready, b + 1)
                need(pool, read["ct"], b)
                for t in range(TT):
                    last = pool.tensor_tensor(coef[:, t, :].rearrange("p (e r) -> p e r", r=RANK),
                                              wide(gating[:, t, :, None], 2, RANK),
                                              wide(rm[:, t, None, EXPERTS:], 1, EXPERTS), ALU.mult)
                last.then_inc(coef_ready, 1)

            def slot(kind, i, at):
                have = parts_of(kind, at)
                if kind == "X":
                    if "M2" in have:
                        scale_qk(i - 1)
                        residual1(1, 0, i - 1)
                        residual2(1, 0, i - 1)
                        residual1(1, 1, i - 1)
                        residual2(1, 1, i - 1)
                    if "P0" in have:
                        apply_norm(0, x_in, i + 1)
                    if "E" in have:
                        normalise(1, i - 2)
                    if "P0" in have:
                        residual1(0, 0, i + 1)
                        residual2(0, 0, i + 1)
                    if "E" in have:
                        apply_norm(3, x3, i - 2)
                    if "P0" in have:
                        residual1(0, 1, i + 1)
                        residual2(0, 1, i + 1)
                    if "E" in have:
                        mix(i - 2)
                else:
                    if at == -1:
                        apply_norm(0, x_in, 0)
                        for n in (0, 1):
                            residual1(0, n, 0)
                            residual2(0, n, 0)
                    if "M1" in have:
                        normalise(0, i)
                        apply_norm(1, x1, i)
                        apply_norm(2, x2, i)
                        square(i)

            walk(pool, slot)

        @block.scalar
        def _(act):
            def copy(dst, src):
                return act.activation(dst, src, ACT.Copy)

            act.wait_ge(w_turned, 1)
            for l in (0, 1):
                copy(wo[l][:, :, :], ps[:, 0, 256 * l:256 * l + 256].rearrange("p (c n) -> p c n", c=2))
            copy(w_gate[:, :, :], ps[:, 1, 0:384].rearrange("p (c n) -> p c n", c=3))
            copy(w_up[:, :, :], ps[:, 2, 0:384].rearrange("p (c n) -> p c n", c=3))
            copy(w_down[:, :, :], ps[:, 3, 0:384].rearrange("p (c n) -> p c n", c=3))
            copy(wqkv[:, :], ps[:, 4, 0:384])
            copy(w_base[:, :], ps[:, 5, 0:128])
            copy(w_mid[:, 0:EXPERTS], ps[:, 5, 128:136]).then_inc(w_ready, 1)

            def exp_unit(l, u, b):
                a = attends_before(l, b)
                act.wait_ge(scores, STEPS * a + u + 1)
                if not (isinstance(a, int) and a == 0 and u < RING):
                    act.wait_ge(pv, 16 * a + u // 2 - RING // 2 + 1)
                act.activation(probs[:, u % RING, :, :], ps[:, 2 * (u % 2):2 * (u % 2) + 2, :], ACT.Exp
                               ).then_inc(exps, 1)

            def save_out(l, half, b):
                act.wait_ge(pv, 16 * attends_before(l, b) + 8 * (half + 1))
                need(act, read[("pr0", "pr1")[l]], b)
                copy(o_raw[l][:, half, :], acc).then_inc(o_saved, 1)

            def take(name, dst, b):
                act.wait_ge(written[name], b + 1)
                copy(dst, gen).then_inc(read[name], 1)

            def take_qk(l, n, b):
                name = (("q0", "k0"), ("qt", "kt"))[l][n]
                act.wait_ge(written[name], b + 1)
                need(act, rows_out[l][n], 48 * b)
                if l == 0:
                    bias = (bq_scaled[:, 0:1], qk_bias[:, 1:2])[n]
                    kw = dict(scale=(QK_SCALE, 1.0)[n], bias=bias)
                else:
                    kw = dict(scale=(qn_scaled[:, 0:1], norm_w[:, 1:2])[n])
                act.activation(qf[l][n][:, :], gen, ACT.Identity, **kw)
                act.activation(qp[l][n][:, 0, :], gen, ACT.Identity, **kw).then_inc(read[name], 1)

            def take_part1(l, n, b):
                act.wait_ge(resid1[2 * l + n], b + 1)
                copy(qp[l][n][:, 1, :], qf[l][n][:, :]).then_inc(part1[2 * l + n], 1)

            def gate_tanh(c, b):
                act.wait_ge(written[f"g{c}"], b + 1)
                act.activation(th[:, :], gen, ACT.Tanh, scale=0.5).then_inc(tanh_done, 1)

            def gate_exp(b):
                act.wait_ge(moe, 3 * (b + 1) + 1 * b)
                act.activation(lexp[:, :, :], lsh[:, :, :], ACT.Exp).then_inc(l_exp, 1)

            def take_coef(b):
                act.wait_ge(written["ct"], b + 1)
                need(act, read["out"], b)
                copy(coef_t[0:EXPERTS * RANK, :], gen[0:EXPERTS * RANK, :]).then_inc(read["ct"], 1)

            def slot(kind, i, at):
                have = parts_of(kind, at)
                if at == -1:
                    act.wait_ge(w_placed, 1)
                    take("xt0", xnt[0][:, :], 0)
                    for n in (0, 1):
                        take_qk(0, n, 0)
                        take_part1(0, n, 0)
                    return
                for s in range(STEPS):
                    if "A" in have:
                        exp_unit(0 if kind == "X" else 1, s, i if kind == "X" else i - 1)
                    if kind == "X":
                        if s == 2 and "At" in have:
                            save_out(1, 1, i - 2)
                        if s == 18 and "A" in have:
                            save_out(0, 0, i)
                        if "M2" in have:
                            if s == 4:
                                take_qk(1, 0, i - 1)
                            if s == 5:
                                take_part1(1, 0, i - 1)
                            if s == 6:
                                take_qk(1, 1, i - 1)
                            if s == 7:
                                take_part1(1, 1, i - 1)
                        if "P0" in have:
                            if s == 9:
                                take("xt0", xnt[0][:, :], i + 1)
                            if s == 11:
                                take_qk(0, 0, i + 1)
                            if s == 13:
                                take_part1(0, 0, i + 1)
                            if s == 15:
                                take_qk(0, 1, i + 1)
                            if s == 19:
                                take_part1(0, 1, i + 1)
                        if "E" in have:
                            if s == 17:
                                take("xt3", xnt[3][:, :], i - 2)
                            if s == 21:
                                gate_exp(i - 2)
                            if s == 23:
                                take_coef(i - 2)
                    else:
                        if s == 2 and "At" in have:
                            save_out(0, 1, i)
                        if s == 18 and "A" in have:
                            save_out(1, 0, i - 1)
                        if "M1" in have:
                            if s == 17:
                                take("xt1", xnt[1][:, :], i)
                            if s in (18, 20, 22):
                                gate_tanh((s - 18) // 2, i)
                            if s == 29:
                                take("xt2", xnt[2][:, :], i)

            walk(act, slot)

        @block.vector
        def _(dve):
            dve.memset(coef_t[64:65, :], 1.0)
            dve.wait_ge(w_loaded, 16 * 24)
            for l in (0, 1):
                dve.memset(v_aug[l][:, :, :, :].rearrange("p a b c -> p (a b c)"), 0.0)
                dve.memset(wo_perm[l], 0.0).then_inc(v_zeros, 1)
            dve.wait_ge(v_zeros, 2)
            for l in (0, 1):
                for c in (0, 1):
                    for s in (0, 1):
                        dst = wo_perm[l][:, 128 * c:128 * c + 128].rearrange("n (pp e s d) -> n e pp s d", pp=2, e=2, s=2)
                        src = wo_nat[l].rearrange("n (e c s pp d) -> n e c s pp d", e=2, c=2, s=2, pp=2)
                        dve.tensor_copy(dst[:, :, :, s, 0:HD], src[:, :, c, s, :, :])
                dve.tensor_copy(wo_perm[l][:, HD:HD + 1], bo_col[l])
                for s in (0, 1):
                    dve.memset(v_aug[l][:, :, :, :].rearrange("p t (r s pp) m -> p (t r) s pp m", s=2, pp=2)
                               [:, :, s, :, 16 * s + HD:16 * s + HD + 1], 1.0)
            for n in range(3):
                dve.tensor_scalar(flt_w[n], int_w[n], DEQUANT, (1.0, 1.0, 0.5)[n], ALU.mult, ALU.mult)
            dve.tensor_scalar(bq_scaled[:, :], qk_bias[:, 0:1], QK_SCALE, None, ALU.mult)
            dve.tensor_scalar(qn_scaled[:, :], norm_w[:, 0:1], QK_SCALE, None, ALU.mult)
            dve.tensor_scalar(w_lora[0:64, :], lora_nat, LORA_SCALE, None, ALU.mult).then_inc(w_placed, 1)

            dve.wait_ge(k_zeros, 6)
            for l in (0, 1):
                k0, k1 = (t[:, :, :].rearrange("p a b -> p (a b)") for t in k_stack[l])
                dve.memset(k0[QROWS:QROWS + MROWS, :], 1.0).then_inc(k_ones, 1)
                dve.memset(k1[QROWS:QROWS + 2 * MROWS, :], 1.0).then_inc(k_both, 1)
                dve.wait_ge(k_both, l + 1)
                dve.memset(k1[QROWS:QROWS + MROWS, :], 0.0).then_inc(k_ones, 1)

            def stats(k, x, b):
                need(dve, xn_ready[k], b)
                for t in range(TT):
                    last = dve.bn_stats(bn[k][:, t, :], x[:, t, :])
                last.then_inc(bn_done[k], 1)
                wait_apart(dve, bn_done[k], b + 1, passed)
                for t in range(TT):
                    last = dve.bn_aggr(mv[k][:, t, :], bn[k][:, t, :])
                last.then_inc(mv_done[k], 1)
                dve.wait_ge(mv_done[k], b + 1)
                dve.tensor_scalar(vpe[k][:, :], mv[k][:, :, 1], LN_EPS, None, ALU.add).then_inc(var_ready[k], 1)

            def stats_in(b):
                dve.wait_ge(x_loaded, 16 * (b + 1))
                stats(0, x_in, b)

            def max_step(l, n, b):
                base = 2 * STEPS * maxima_before(l, b) + 2 * n
                pair, st = n // 4, n % 4
                for e in (0, 1):
                    dve.wait_ge(max_scores, base + e + 1)
                    col = 4 * e + pair % 4
                    dve.tensor_reduce(neg_max[l][:, pair // 4, st, col:col + 1], ps[:, 4 + e, :], AX.X, ALU.max,
                                      negate=True).then_inc(max_taken, 1)

            def split_max(l, half, b):
                name = f"m{l}{'ab'[half]}"
                dve.wait_ge(written[name], b + 1)
                need(dve, m_in[l][half], 64 * b)
                dve.tensor_copy(m_parts[l][half][:, 0, :], gen[0:8, :]).then_inc(m_part0[l][half], 1)
                dve.wait_ge(m_part0[l][half], b + 1)
                dve.tensor_tensor(m_parts[l][half][:, 1, :], gen[0:8, :], m_parts[l][half][:, 0, :], ALU.subtract
                                  ).then_inc(read[name], 1)

            def take_v(l, b):
                name = ("v0", "v1")[l]
                dve.wait_ge(written[name], b + 1)
                src = gen.rearrange("p (r s m) -> p r s m", s=2, m=2 * HD)
                bias = v_bias[l][:, :].rearrange("p (r s m) -> p r s m", s=2, m=2 * HD)
                dst = v_aug[l][:, :, :, :].rearrange("p t (r s pp) m -> p (t r) s pp m", s=2, pp=2)
                for t in range(TT):
                    for s in (0, 1):
                        last = dve.tensor_tensor(
                            dst[:, 4 * t:4 * t + 4, s, :, 16 * s:16 * s + HD],
                            src[:, 4 * t:4 * t + 4, s, :].rearrange("p r (pp d) -> p r pp d", d=HD),
                            bias[:, :, s, :].rearrange("p r (pp d) -> p r pp d", d=HD), ALU.add)
                last.then_inc(read[name], 1)

            def invert_den(l, b):
                dve.wait_ge(den_in[l], 16 * (b + 1))
                need(dve, rden_out[l], 16 * b)
                dve.reciprocal(rden[l][:, :], den[l][:, :]).then_inc(rden_ready[l], 1)

            def add_into(name, dst, other, b):
                dve.wait_ge(written[name], b + 1)
                dve.tensor_tensor(dst[:, :, :], gen4, other[:, :, :], ALU.add).then_inc(read[name], 1)

            def project_add(l, dst, b):
                dve.wait_ge(res_copied[l], 16 * (b + 1))
                if l == 1:
                    need(dve, stored, 16 * b)
                add_into(("pr0", "pr1")[l], dst, res[l], b)
                dve.wait_ge(read[("pr0", "pr1")[l]], b + 1)
                stats((1, 3)[l], dst, b)

            def gate_mul(c, b):
                dve.wait_ge(tanh_done, NH * b + c + 1)
                dve.scalar_tensor_tensor(out=gs[:, :], in0=th[:, :], scalar=1.0, in1=gen, op0=ALU.add,
                                         op1=ALU.mult).then_inc(read[f"g{c}"], 1)

            def up_mul(c, b):
                dve.wait_ge(written[f"u{c}"], b + 1)
                dve.tensor_tensor(ht[:, c, :], gen, gs[:, :], ALU.mult).then_inc(read[f"u{c}"], 1)

            def down_add(b):
                need(dve, res_copied[1], 16 * b)
                add_into("dn", x2, x1, b)
                dve.wait_ge(read["dn"], b + 1)
                stats(2, x2, b)

            def take_qk1(half, b):
                name = ("qka", "qkb")[half]
                dve.wait_ge(written[name], b + 1)
                for t in (0, 1):
                    last = dve.tensor_tensor(qk1[:, 2 * half + t, :], gen[:, 256 * t:256 * t + 256], qk1_bias[:, :], ALU.add)
                last.then_inc(read[name], 1)

            def inverse_rms(b):
                at = [N_NEWTON * b]

                def link(ins, wait=True):
                    at[0] = at[0] + 1
                    ins.then_inc(newton, 1)
                    if wait:
                        dve.wait_ge(newton, at[0])

                dve.wait_ge(squared, b + 1)
                link(dve.tensor_reduce(ms[:, :], sq[:, :, :].rearrange("p t (g e) -> p (t g) e", e=HD), AX.X, ALU.add))
                link(dve.tensor_scalar(ms[:, :], ms[:, :], 1.0 / HD, RMS_EPS, ALU.mult, ALU.add))
                link(dve.tensor_scalar(nw_t[:, :].bitcast(I32), ms[:, :].bitcast(I32), 1, None, ALU.logical_shift_right))
                link(dve.tensor_scalar(nw_y[:, :].bitcast(I32), nw_t[:, :].bitcast(I32), -1.0, float(0x5f3759df),
                                       ALU.mult, ALU.add))
                for k in range(3):
                    link(dve.tensor_tensor(nw_t[:, :], nw_y[:, :], nw_y[:, :], ALU.mult))
                    link(dve.scalar_tensor_tensor(out=nw_u[:, :], in0=nw_t[:, :], scalar=-0.5, in1=ms[:, :],
                                                  op0=ALU.mult, op1=ALU.mult))
                    link(dve.scalar_tensor_tensor(out=nw_y[:, :], in0=nw_u[:, :], scalar=1.5, in1=nw_y[:, :],
                                                  op0=ALU.add, op1=ALU.mult), wait=k < 2)

            def route(b):
                dve.wait_ge(written["rt"], b + 1)
                at = 4 * b
                dve.tensor_tensor(rm[:, :, :], gen[:, 0:TT * 16].rearrange("p (t n) -> p t n", t=TT),
                                  wide(mid_bias[:, None, :], 1, TT), ALU.add).then_inc(read["rt"], 1)
                dve.wait_ge(read["rt"], b + 1)
                dve.tensor_reduce(lmax[:, :], rm[:, :, 0:EXPERTS], AX.X, ALU.max).then_inc(moe, 2)
                dve.wait_ge(moe, at + 2)
                dve.tensor_tensor(lsh[:, :, :], rm[:, :, 0:EXPERTS], wide(lmax[:, :, None], 2, EXPERTS),
                                  ALU.subtract).then_inc(moe, 1)

            def gates(b):
                dve.wait_ge(l_exp, b + 1)
                dve.tensor_reduce(lsum[:, :], lexp[:, :, :], AX.X, ALU.add).then_inc(moe, 1)
                dve.wait_ge(moe, 4 * b + 4)
                dve.reciprocal(lrec[:, :], lsum[:, :]).then_inc(m_rec, 1)
                dve.wait_ge(m_rec, b + 1)
                dve.tensor_tensor(gating[:, :, :], lexp[:, :, :], wide(lrec[:, :, None], 2, EXPERTS), ALU.mult
                                  ).then_inc(gate_ready, 1)

            def finish(b):
                add_into("out", x3, x3, b)

            def slot(kind, i, at):
                have = parts_of(kind, at)
                if at == -1:
                    stats_in(0)
                tail, head = ((0, i), (1, i - 1)) if kind == "X" else ((1, i - 1), (0, i + 1))
                for s in range(STEPS):
                    if at == -1 and s == 6:
                        take_v(0, 0)
                    if s < LEAD and "MXt" in have:
                        max_step(tail[0], s + STEPS - LEAD, tail[1])
                    if s >= LEAD and "MXh" in have:
                        max_step(head[0], s - LEAD, head[1])
                    if s == 12 and "MXt" in have:
                        split_max(tail[0], 1, tail[1])
                    if s == 28 and "MXh" in have:
                        split_max(head[0], 0, head[1])
                    if kind == "X":
                        if "M2" in have:
                            if s == 0:
                                inverse_rms(i - 1)
                            if s == 8:
                                take_v(1, i - 1)
                        if "P0" in have and s == 4:
                            stats_in(i + 1)
                        if "E" in have:
                            if s == 6:
                                invert_den(1, i - 2)
                            if s == 13:
                                project_add(1, x3, i - 2)
                            if s == 19:
                                route(i - 2)
                            if s == 21:
                                gates(i - 2)
                            if s == 25:
                                finish(i - 2)
                    else:
                        if s == 6 and "V0" in have and at >= 0:
                            take_v(0, i + 1)
                        if "M1" in have:
                            if s == 6:
                                invert_den(0, i)
                            if s == 13:
                                project_add(0, x1, i)
                            if s in (18, 20, 22):
                                gate_mul((s - 18) // 2, i)
                            if s in (19, 21, 23):
                                up_mul((s - 19) // 2, i)
                            if s == 24:
                                down_add(i)
                            if s == 30:
                                take_qk1(0, i)
                            if s == 31:
                                take_qk1(1, i)

            walk(dve, slot)

        @block.tensor
        def _(pe):
            def turn(dst, src, n=128):
                return pe.transpose(dst, src, ident[0:n, 0:n])

            pe.wait_ge(ident_ready, 1)
            pe.wait_ge(w_placed, 1)
            for l in (0, 1):
                for c in (0, 1):
                    turn(ps[:, 0, 256 * l + 128 * c:256 * l + 128 * c + 128], wo_perm[l][:, 128 * c:128 * c + 128])
            for n, w in enumerate((flt_w[0], flt_w[1], flt_w[2], wqkv_nat)):
                for c in range(3):
                    turn(ps[:, 1 + n, 128 * c:128 * c + 128], w[:, 128 * c:128 * c + 128])
            turn(ps[:, 5, 0:128], base_nat)
            turn(ps[:, 5, 128:128 + EXPERTS], router_nat, EXPERTS).then_inc(w_turned, 1)
            pe.wait_ge(w_ready, 1)
            pe.wait_ge(k_ones, 4)

            def max_score(l, n, e, b):
                base = 2 * STEPS * maxima_before(l, b) + 2 * n
                if e == 0 and n % 16 == 0:
                    pe.wait_ge(stack_in[l][n // 16], 64 * (b + 1))
                need(pe, max_taken, base + e - 1)
                tok, pair = 128 * (n % 4), n // 4
                pe.matmul(ps[:, 4 + e, :], q_stack[l][0:QROWS, pair, tok:tok + 128], k_stack[l][e][0:QROWS, pair, :],
                          start=True, stop=True).then_inc(max_scores, 1)

            def attend_score(l, u, e, b):
                group, kt, pp = u // 8, (u % 8) // 2, u % 2
                if e == 0:
                    if u % 16 == 0:
                        pe.wait_ge(m_in[l][u // 16], 64 * (b + 1))
                    need(pe, exps, STEPS * attends_before(l, b) + u - 1)
                tok, pair = 128 * kt, 2 * group + pp
                last = pe.matmul(ps[:, 2 * (u % 2) + e, :], k_stack[l][e][:, pair, tok:tok + 128],
                                 q_stack[l][:, pair, :], start=True, stop=True)
                if e == 1:
                    last.then_inc(scores, 1)

            def attend_pv(l, u, b):
                group, kt = u // 8, (u % 8) // 2
                c, s = group // 2, group % 2
                a = attends_before(l, b)
                if u == 0:
                    pe.wait_ge(read[("v0", "v1")[l]], b + 1)
                if u % 16 == 0:
                    need(pe, o_saved, 2 * a + c)
                pe.wait_ge(exps, STEPS * a + u + 2)
                for pp in (0, 1):
                    for e in (0, 1):
                        j = 2 * pp + e
                        last = pe.matmul(acc[32 * j:32 * j + 32, :], v_aug[l][:, kt, 8 * e + 2 * group + pp, :],
                                         probs[:, (u + pp) % RING, e, :], start=(s == 0 and kt == 0),
                                         stop=(s == 1 and kt == TT - 1))
                last.then_inc(pv, 1)

            def turn_norm(k, b):
                pe.wait_ge(xn_ready[k], b + 1)
                for t in range(TT):
                    last = turn(gen[:, 128 * t:128 * t + 128], xn[k][:, t, :])
                return last

            def turn_max(l, half):
                for st in range(TT):
                    last = turn(gen[0:8, 128 * st:128 * st + 128], neg_max[l][:, half, st, :])
                return last

            def by_token(dst, xt, w, more=None):
                for t in range(TT):
                    last = pe.matmul(dst[:, t, :], xt[:, 128 * t:128 * t + 128], w, start=True, stop=more is None)
                    if more is not None:
                        last = pe.matmul(dst[:, t, :], more[0][:, 128 * t:128 * t + 128], more[1], start=False, stop=True)
                return last

            def project(l, b):
                pe.wait_ge(att_ready[l], b + 1)
                for t in range(TT):
                    for c in (0, 1):
                        last = pe.matmul(gen4[:, t, :], o_raw[l][:, c, 128 * t:128 * t + 128], wo[l][:, c, :],
                                         start=c == 0, stop=c == 1)
                return last

            def piece(name, i, at, kind, b):
                before = piece_before(kind, at, name)
                if before is not None:
                    pe.wait_ge(read[before[0]], i + before[1] + 1)
                if name in ("xt0", "xt1", "xt2", "xt3"):
                    last = turn_norm(int(name[2]), b)
                elif name in ("q0", "k0"):
                    pe.wait_ge(read["xt0"], b + 1)
                    last = pe.matmul(gen, (wq if name == "q0" else wk)[:, :], xnt[0][:, :], start=True, stop=True)
                elif name == "v0":
                    pe.wait_ge(read["xt0"], b + 1)
                    last = by_token(gen4, xnt[0], wv[:, :])
                elif name == "v1":
                    last = by_token(gen4, xnt[2], wqkv[:, 256:384])
                elif name in ("m0a", "m0b", "m1a", "m1b"):
                    l, half = int(name[1]), "ab".index(name[2])
                    pe.wait_ge(max_taken, 2 * STEPS * maxima_before(l, b) + STEPS * (half + 1))
                    last = turn_max(l, half)
                elif name in ("pr0", "pr1"):
                    last = project(int(name[2]), b)
                elif name[0] in "gu":
                    pe.wait_ge(read["xt1"], b + 1)
                    w = w_gate if name[0] == "g" else w_up
                    last = pe.matmul(gen, w[:, int(name[1]), :], xnt[1][:, :], start=True, stop=True)
                elif name == "dn":
                    for t in range(TT):
                        for c in range(NH):
                            last = pe.matmul(gen4[:, t, :], ht[:, c, 128 * t:128 * t + 128], w_down[:, c, :],
                                             start=c == 0, stop=c == NH - 1)
                elif name in ("qka", "qkb"):
                    pe.wait_ge(read["xt2"], b + 1)
                    half = int(name == "qkb")
                    for t in (0, 1):
                        tok = 128 * (2 * half + t)
                        last = pe.matmul(gen[:, 256 * t:256 * t + 256], xnt[2][:, tok:tok + 128], wqkv[:, 0:256],
                                         start=True, stop=True)
                elif name in ("qt", "kt"):
                    if name == "qt":
                        pe.wait_ge(qk_normed, b + 1)
                    for t in range(TT):
                        c = 128 * (name == "kt")
                        last = turn(gen[:, 128 * t:128 * t + 128], qk1[:, t, c:c + 128])
                elif name == "rt":
                    pe.wait_ge(read["xt3"], b + 1)
                    last = by_token(gen[:, 0:TT * 16].rearrange("p (t n) -> p t n", t=TT), xnt[3], w_mid[:, :])
                elif name == "ct":
                    wait_apart(pe, coef_ready, b + 1, passed)
                    for t in range(TT):
                        last = turn(gen[0:64, 128 * t:128 * t + 128], coef[:, t, :])
                elif name == "out":
                    last = by_token(gen4, xnt[3], w_base[:, :], more=(coef_t, w_lora[:, :]))
                last.then_inc(written[name], 1)

            def slot(kind, i, at):
                have = parts_of(kind, at)
                pieces = slot_pieces(kind, at)
                if at == -1:
                    for name in ("xt0", "q0", "k0", "v0"):
                        if name == "xt0":
                            last = turn_norm(0, 0)
                        elif name == "v0":
                            pe.wait_ge(read["k0"], 1)
                            last = by_token(gen4, xnt[0], wv[:, :])
                        else:
                            pe.wait_ge(read["xt0" if name == "q0" else "q0"], 1)
                            last = pe.matmul(gen, (wq if name == "q0" else wk)[:, :], xnt[0][:, :], start=True, stop=True)
                        last.then_inc(written[name], 1)
                    pieces = [p for p in pieces if p[1] != "v0"]
                tail, head = ((0, i), (1, i - 1)) if kind == "X" else ((1, i - 1), (0, i + 1))
                now, past = ((0, i), (1, i - 2)) if kind == "X" else ((1, i - 1), (0, i))
                for s in range(STEPS):
                    mx = None
                    if s < LEAD and "MXt" in have:
                        mx = (tail[0], s + STEPS - LEAD, tail[1])
                    if s >= LEAD and "MXh" in have:
                        mx = (head[0], s - LEAD, head[1])
                    if mx:
                        max_score(mx[0], mx[1], 0, mx[2])
                    if "A" in have:
                        attend_score(now[0], s, 0, now[1])
                        attend_score(now[0], s, 1, now[1])
                    if mx:
                        max_score(mx[0], mx[1], 1, mx[2])
                    if s == 1 and "At" in have:
                        attend_pv(past[0], STEPS - 2, past[1])
                    if s % 2 and s > 1 and "A" in have:
                        attend_pv(now[0], s - 3, now[1])
                    for at_step, name in pieces:
                        if at_step == s:
                            piece(name, i, at, kind, i + PIECE[name][0])

            walk(pe, slot)


NAMES = ["L0_attn_x", "L0_attn_wq", "L0_attn_bq", "L0_attn_wk", "L0_attn_bk", "L0_attn_wv", "L0_attn_bv",
         "L0_attn_wo", "L0_attn_bo", "L0_ffn_w_gate", "L0_ffn_w_up", "L0_ffn_w_down", "L1_attn_Wqkv",
         "L1_attn_bqkv", "L1_attn_Wproj", "L1_attn_bproj", "L1_attn_qn_w", "L1_attn_kn_w", "L1_ffn_base_w",
         "L1_ffn_base_b", "L1_ffn_lora_A", "L1_ffn_lora_B", "L1_ffn_router_w", "L1_ffn_router_b"]


def kernel(**inputs):
    import numpy as _np
    import concourse.bacc as _bacc
    from concourse import mybir as _mybir
    from concourse.bass_utils import run_bass_kernel_spmd as _run

    nc = _bacc.Bacc("TRN2", target_bir_lowering=False, num_devices=1)
    arrays, tensors = {}, {}
    for name in NAMES:
        a = _np.ascontiguousarray(inputs[name])
        arrays[f"in_{name}"] = a
        tensors[name] = nc.dram_tensor(f"in_{name}", a.shape, _mybir.dt.from_np(a.dtype), kind="ExternalInput").ap()
    out = nc.dram_tensor("out_x", (BATCH, SEQ, D), F32, kind="ExternalOutput").ap()
    build(nc, tensors, out)
    r = _run(nc, [arrays], core_ids=[0])
    return r.results[0]["out_x"]
```

```python
import numpy as np
import concourse.bass as bass
from concourse import mybir
from contextlib import ExitStack

F32 = mybir.dt.float32
BF16 = mybir.dt.bfloat16
I32 = mybir.dt.int32
ALU = mybir.AluOpType
ACT = mybir.ActivationFunctionType
AX = mybir.AxisListType

BATCH, SEQ, D = 16, 512, 128
HEADS, HD = 16, 8
HID = 384
TT = SEQ // 128
NH = HID // 128
EXPERTS, RANK = 8, 8
LORA_SCALE = 2.0
DEQUANT = float(np.float32(1.0 / 127.0))
QK_SCALE = float(1.0 / np.sqrt(HD))
LN_EPS, RMS_EPS = 1e-5, 1e-6

PAIRS = HEADS // 2
PARTS = 3
TERMS = 6
Q_PART = (0, 0, 0, 1, 1, 2)
K_PART = (0, 1, 2, 0, 1, 0)
KROWS = HD * TERMS
MROWS = 2
QROWS = 2 * KROWS

STEPS = 32
LEAD = 18
UNITS = 2 * STEPS
RING = 16
SCORE_BANKS = 3
MAX_BANKS = 3

X_PE = ((2, "m01"), (4, "v1"), (7, "qt"), (8, "kt"), (11, "m02"), (16, "pr1"), (17, "xt0"),
        (18, "m03"), (19, "q0"), (21, "k0"), (22, "xt3"), (24, "rt"), (26, "m10"), (28, "ct"), (30, "out"))
Y_PE = ((2, "m11"), (5, "v0"), (10, "pr0"), (11, "m12"), (13, "xt1"), (14, "g0"), (15, "u0"), (16, "g1"),
        (17, "u1"), (18, "m13"), (20, "g2"), (21, "u2"), (23, "dn"), (26, "m00"), (27, "xt2"), (28, "qka"),
        (29, "qkb"))
PIECE = {"qt": (-1, "M2"), "kt": (-1, "M2"), "v1": (-1, "M2"),
         "xt0": (1, "P0"), "q0": (1, "P0"), "k0": (1, "P0"), "v0": (1, "V0"),
         "pr1": (-2, "E"), "xt3": (-2, "E"), "rt": (-2, "E"), "ct": (-2, "E"), "out": (-2, "E"),
         "m01": (0, "MXt"), "m02": (0, "MXt"), "m03": (0, "MXt"), "m10": (-1, "MXh"),
         "m11": (-1, "MXt"), "m12": (-1, "MXt"), "m13": (-1, "MXt"), "m00": (1, "MXh"),
         "pr0": (0, "M1"), "xt1": (0, "M1"), "g0": (0, "M1"), "u0": (0, "M1"), "g1": (0, "M1"), "u1": (0, "M1"),
         "g2": (0, "M1"), "u2": (0, "M1"), "dn": (0, "M1"), "xt2": (0, "M1"), "qka": (0, "M1"), "qkb": (0, "M1")}


def sem_name(piece):
    return piece[0:2] if piece[0] == "m" else piece


def count(piece, b):
    return 4 * b + int(piece[2]) + 1 if piece[0] == "m" else b + 1


def parts_of(kind, i):
    if kind == "X":
        have = (("A", i < BATCH), ("At", 1 <= i - 1 + 0 and i - 2 >= 0), ("MXt", i < BATCH),
                ("MXh", 1 <= i <= BATCH), ("M2", 1 <= i <= BATCH), ("P0", i + 1 < BATCH), ("E", i >= 2))
    else:
        have = (("A", 1 <= i <= BATCH), ("At", 0 <= i < BATCH), ("MXt", 1 <= i <= BATCH),
                ("MXh", i + 1 < BATCH), ("M1", 0 <= i < BATCH), ("V0", i + 1 < BATCH))
    return frozenset(n for n, yes in have if yes)


def slot_pieces(kind, i):
    have = parts_of(kind, i)
    return [(s, n) for s, n in (X_PE if kind == "X" else Y_PE) if PIECE[n][1] in have]


M_TAIL = (2, 11, 18)
M_HEAD = 26
SLOTS = [("Y", -1)] + [(k, i) for i in range(BATCH + 2) for k in "XY" if (k, i) != ("Y", BATCH + 1)]
LOOP_FROM, LOOP_TO = 2, BATCH - 1
assert all(parts_of("X", i) == parts_of("X", 2) and parts_of("Y", i - 1) == parts_of("Y", 2)
           for i in range(LOOP_FROM, LOOP_TO))


def piece_before(kind, i, name):
    seen = []
    for k, j in SLOTS:
        for _, n in slot_pieces(k, j):
            if (k, j, n) == (kind, i, name):
                return (seen[-1][0], seen[-1][1] - i) if seen else None
            seen.append((n, j + PIECE[n][0]))
    raise AssertionError(name)


def attends_before(layer, b):
    if isinstance(b, int):
        return (max(2 * b - 1, 0) if layer == 0 else min(2 * b + 2, 2 * BATCH - 1))
    return 2 * b - 1 if layer == 0 else 2 * b + 2


def maxima_before(layer, b):
    return attends_before(layer, b)


def bank_of(layer, n):
    return (n + layer) % 3


def free_at(layer, n, b, base):
    if isinstance(b, int) and n == 0 and (layer, b) in ((0, 1), (1, BATCH - 1)):
        return base
    if layer == 0 and n < 2:
        return base + n - 1
    return base + n - 2


def wide(ap, dim, n):
    shape = list(ap.shape)
    shape[dim] = n
    return ap.broadcast_to(shape)


def need(eng, sem, value):
    if isinstance(value, int) and value <= 0:
        return
    eng.wait_ge(sem, value)


def wait_apart(eng, sem, value, passed):
    need(eng, sem, value)
    if not isinstance(value, int):
        eng.sem_inc(passed, 1)


def build(nc, T, out_dram):
    ctx = ExitStack()
    with ctx:
        def sb(name, shape, dt=F32):
            return ctx.enter_context(nc.sbuf_tensor(name, shape, dt))

        def sem(name):
            return ctx.enter_context(nc.semaphore(name))

        q_rows = [nc.dram_tensor(f"q_rows{l}", (128, TERMS, SEQ), BF16).ap() for l in (0, 1)]
        k_rows = [nc.dram_tensor(f"k_rows{l}", (128, TERMS, SEQ), BF16).ap() for l in (0, 1)]
        rden_rows = [nc.dram_tensor(f"rden_rows{l}", (8, 2 * SEQ), F32).ap() for l in (0, 1)]

        ident = sb("ident", [128, 128])
        wq = sb("wq", [128, D])
        wk = sb("wk", [128, D])
        wv = sb("wv", [128, D])
        qk_bias = sb("qk_bias", [128, 2])
        bq_scaled = sb("bq_scaled", [128, 1])
        v_bias = [sb(f"v_bias{l}", [128, D]) for l in (0, 1)]
        wo = [sb(f"wo{l}", [128, 2, D]) for l in (0, 1)]
        w_gate = sb("w_gate", [128, NH, 128])
        w_up = sb("w_up", [128, NH, 128])
        w_down = sb("w_down", [128, NH, D])
        wqkv = sb("wqkv", [128, 3 * D])
        qk1_bias = sb("qk1_bias", [128, 2 * D])
        norm_w = sb("norm_w", [128, 2])
        qn_scaled = sb("qn_scaled", [128, 1])
        w_base = sb("w_base", [128, D])
        w_mid = sb("w_mid", [128, 2 * EXPERTS])
        mid_bias = sb("mid_bias", [128, 2 * EXPERTS])
        w_lora = sb("w_lora", [EXPERTS * RANK + 1, D])
        half_neg = sb("half_neg", [128, TT])

        x_in = sb("x_in", [128, TT, D])
        res = [sb(f"res{l}", [128, TT, D]) for l in (0, 1)]
        x1 = sb("x1", [128, TT, D])
        x2 = sb("x2", [128, TT, D])
        x3 = sb("x3", [128, TT, D])
        bn = [sb(f"bn{k}", [128, TT, 6]) for k in range(4)]
        mv = [sb(f"mv{k}", [128, TT, 2]) for k in range(4)]
        vpe = [sb(f"vpe{k}", [128, TT]) for k in range(4)]
        rstd = [sb(f"rstd{k}", [128, TT]) for k in range(4)]
        neg_mean = [sb(f"neg_mean{k}", [128, TT]) for k in range(4)]
        shift = [sb(f"shift{k}", [128, TT]) for k in range(4)]
        xn = [sb(f"xn{k}", [128, TT, D]) for k in (0, 1, 3)]
        xn.insert(2, xn[1])
        xnt = [sb(f"xnt{k}", [128, SEQ]) for k in range(4)]

        qf = [[sb(f"{c}f{l}", [128, SEQ]) for c in "qk"] for l in (0, 1)]
        qp = [[sb(f"{c}p{l}", [128, PARTS, SEQ], BF16) for c in "qk"] for l in (0, 1)]
        q_stack = [sb(f"q_stack{l}", [128, PAIRS, SEQ], BF16) for l in (0, 1)]
        k_stack = [[sb(f"k_stack{l}{e}", [128, PAIRS, SEQ], BF16) for e in (0, 1)] for l in (0, 1)]
        v_aug = [sb(f"v_aug{l}", [128, TT, HEADS, 32]) for l in (0, 1)]
        neg_max = [sb(f"neg_max{l}", [128, 4, 32]) for l in (0, 1)]
        neg_high = [sb(f"neg_high{l}", [128, 4, 16], BF16) for l in (0, 1)]
        m_parts = [[sb(f"m_parts{l}{k}", [32, 128], BF16) for k in (0, 1)] for l in (0, 1)]
        probs = sb("probs", [128, RING, SEQ])
        o_raw = [sb(f"o_raw{l}", [128, 2, SEQ]) for l in (0, 1)]
        rden_all = [sb(f"rden_all{l}", [128, 2, SEQ]) for l in (0, 1)]
        den = [sb(f"den{l}", [128, 64]) for l in (0, 1)]
        rden = [sb(f"rden{l}", [128, 64]) for l in (0, 1)]

        th = sb("th", [128, SEQ])
        gs = sb("gs", [128, SEQ])
        ht = sb("ht", [128, NH, SEQ])
        qk1 = sb("qk1", [128, TT, 2 * D])
        sq = ht[:, 0:2, :].rearrange("p c (t n) -> p (c t) n", n=2 * D)
        ms = sb("ms", [128, TT * 32])
        nw_y = sb("nw_y", [128, TT * 32])
        nw_t = sb("nw_t", [128, TT * 32])
        nw_u = sb("nw_u", [128, TT * 32])

        rm = sb("rm", [128, TT, 2 * EXPERTS])
        lmax = sb("lmax", [128, TT])
        lsh = sb("lsh", [128, TT, EXPERTS])
        lexp = sb("lexp", [128, TT, EXPERTS])
        lsum = sb("lsum", [128, TT])
        lrec = sb("lrec", [128, TT])
        gating = sb("gating", [128, TT, EXPERTS], BF16)
        coef = sb("coef", [128, TT, EXPERTS * RANK])
        coef_t = sb("coef_t", [EXPERTS * RANK + 1, SEQ])

        stage = probs[:, :, :].rearrange("p a b -> p (a b)")
        wo_nat = [stage[:, l * 128:(l + 1) * 128] for l in (0, 1)]
        wo_perm = [stage[:, 256 + l * 256:512 + l * 256] for l in (0, 1)]
        bo_col = [stage[:, 768 + l:769 + l] for l in (0, 1)]
        int_w = [stage[:, 1024 + 384 * n:1408 + 384 * n].bitcast(I32) for n in range(3)]
        flt_w = [stage[:, 2304 + 384 * n:2688 + 384 * n] for n in range(3)]
        wqkv_nat = stage[:, 3584:3968]
        base_nat = stage[:, 3968:4096]
        router_nat = stage[0:EXPERTS, 4096:4224]
        lora_nat = stage[0:EXPERTS * RANK, 4224:4352]

        ps = ctx.enter_context(nc.psum_tensor("ps", [128, 8, 512], F32))
        acc = ps[:, 6, :]
        gen = ps[:, 7, :]
        gen4 = gen.rearrange("p (t n) -> p t n", t=TT)

        w_loaded = sem("w_loaded")
        k_zeros = sem("k_zeros")
        k_both = sem("k_both")
        k_ones = sem("k_ones")
        v_zeros = sem("v_zeros")
        ident_zero = sem("ident_zero")
        ident_ready = sem("ident_ready")
        w_placed = sem("w_placed")
        w_turned = sem("w_turned")
        w_ready = sem("w_ready")
        names = sorted({sem_name(n) for n in PIECE})
        written = {n: sem(f"{n}_written") for n in names}
        read = {n: sem(f"{n}_read") for n in names}
        x_loaded = sem("x_loaded")
        res_copied = [sem(f"res_copied{l}") for l in (0, 1)]
        bn_done = [sem(f"bn_done{k}") for k in range(4)]
        mv_done = [sem(f"mv_done{k}") for k in range(4)]
        var_ready = [sem(f"var_ready{k}") for k in range(4)]
        rstd_ready = [sem(f"rstd_ready{k}") for k in range(4)]
        shift_ready = [sem(f"shift_ready{k}") for k in range(4)]
        xn_ready = [sem(f"xn_ready{k}") for k in range(4)]
        resid1 = [sem(f"{c}_resid1") for c in ("q0", "k0", "q1", "k1")]
        part1 = [sem(f"{c}_part1") for c in ("q0", "k0", "q1", "k1")]
        part2 = [sem(f"{c}_part2") for c in ("q0", "k0", "q1", "k1")]
        rows_out = [[sem(f"{c}rows_out{l}") for c in "qk"] for l in (0, 1)]
        stack_in = [[sem(f"stack_in{l}{h}") for h in (0, 1)] for l in (0, 1)]
        high_done = sem("high_done")
        low_done = [sem(f"low_done{l}") for l in (0, 1)]
        m_in = [[sem(f"m_in{l}{q}") for q in range(4)] for l in (0, 1)]
        max_scores = sem("max_scores")
        max_taken = sem("max_taken")
        scores = sem("scores")
        exps = sem("exps")
        pv = sem("pv")
        o_saved = sem("o_saved")
        den_in = [sem(f"den_in{l}") for l in (0, 1)]
        rden_ready = [sem(f"rden_ready{l}") for l in (0, 1)]
        rden_out = [sem(f"rden_out{l}") for l in (0, 1)]
        rden_in = [sem(f"rden_in{l}") for l in (0, 1)]
        att_ready = [sem(f"att_ready{l}") for l in (0, 1)]
        tanh_done = sem("tanh_done")
        squared = sem("squared")
        newton = sem("newton")
        qk_normed = [sem(f"{c}_normed") for c in "qk"]
        moe = sem("moe")
        l_exp = sem("l_exp")
        m_rec = sem("m_rec")
        gate_ready = sem("gate_ready")
        coef_ready = sem("coef_ready")
        stored = sem("stored")
        passed = sem("passed")
        N_NEWTON = 14

        block = ctx.enter_context(nc.Block())

        def walk(eng, slot):
            for k, i in SLOTS:
                if LOOP_FROM <= i < LOOP_TO:
                    if (k, i) == ("X", LOOP_FROM):
                        with eng.Fori(LOOP_FROM, LOOP_TO) as it:
                            slot("X", it, LOOP_FROM)
                            slot("Y", it, LOOP_FROM)
                else:
                    slot(k, i, i)

        @block.sync
        def _(sp):
            def hold(sem, value):
                wait_apart(sp, sem, value, passed)

            def load(dst, src):
                sp.dma_start(dst, src).then_inc(w_loaded, 16)

            sp.dma_start(x_in[:, :, :], T["L0_attn_x"][0].rearrange("(t p) d -> p t d", p=128)).then_inc(x_loaded, 16)
            load(wq[:, :].rearrange("d (h e) -> d h e", h=HEADS), T["L0_attn_wq"].rearrange("h d e -> d h e"))
            load(wk[:, :].rearrange("d (h e) -> d h e", h=HEADS), T["L0_attn_wk"].rearrange("h d e -> d h e"))
            load(wv[:, :].rearrange("d (h e) -> d h e", h=HEADS), T["L0_attn_wv"].rearrange("h d e -> d h e"))
            load(qk_bias[:, 0:1], bass.AP(T["L0_attn_bq"].tensor, 0, [[1, 128], [1, 1]]))
            load(qk_bias[:, 1:2], bass.AP(T["L0_attn_bk"].tensor, 0, [[1, 128], [1, 1]]))
            load(v_bias[0][:, :], bass.AP(T["L0_attn_bv"].tensor, 0, [[0, 128], [1, 128]]))
            load(wo_nat[0], T["L0_attn_wo"])
            load(wo_nat[1], T["L1_attn_Wproj"])
            load(bo_col[0], bass.AP(T["L0_attn_bo"].tensor, 0, [[1, 128], [1, 1]]))
            load(bo_col[1], bass.AP(T["L1_attn_bproj"].tensor, 0, [[1, 128], [1, 1]]))
            load(int_w[0].rearrange("p (c f) -> p c f", c=NH), T["L0_ffn_w_gate"].rearrange("(c p) f -> p c f", p=128))
            load(int_w[1].rearrange("p (c f) -> p c f", c=NH), T["L0_ffn_w_up"].rearrange("(c p) f -> p c f", p=128))
            load(int_w[2], T["L0_ffn_w_down"])
            load(wqkv_nat.rearrange("p (c f) -> p c f", c=3), T["L1_attn_Wqkv"].rearrange("(c p) f -> p c f", p=128))
            load(qk1_bias[:, :], bass.AP(T["L1_attn_bqkv"].tensor, 0, [[0, 128], [1, 256]]))
            load(v_bias[1][:, :], bass.AP(T["L1_attn_bqkv"].tensor, 256, [[0, 128], [1, 128]]))
            load(norm_w[:, 0:1], bass.AP(T["L1_attn_qn_w"].tensor, 0, [[0, HEADS], [1, HD], [1, 1]]))
            load(norm_w[:, 1:2], bass.AP(T["L1_attn_kn_w"].tensor, 0, [[0, HEADS], [1, HD], [1, 1]]))
            load(base_nat, T["L1_ffn_base_w"])
            load(router_nat, T["L1_ffn_router_w"])
            load(w_mid[:, EXPERTS:], T["L1_ffn_lora_A"])
            load(lora_nat, T["L1_ffn_lora_B"].rearrange("e r d -> (e r) d"))
            load(w_lora[64:65, :], bass.AP(T["L1_ffn_base_b"].tensor, 0, [[0, 1], [1, 128]]))
            load(mid_bias[:, 0:EXPERTS], bass.AP(T["L1_ffn_router_b"].tensor, 0, [[0, 128], [1, 8]]))
            hold(x_loaded, 16)
            sp.dma_start(res[0][:, :, :], x_in[:, :, :]).then_inc(res_copied[0], 16)

            def load_x(b):
                hold(xn_ready[0], b)
                hold(res_copied[0], 16 * b)
                src = T["L0_attn_x"][bass.ds(b, 1)] if not isinstance(b, int) else T["L0_attn_x"][b:b + 1]
                sp.dma_start(x_in[:, :, :], src.rearrange("a (t p) d -> p (a t) d", p=128)).then_inc(x_loaded, 16)

            def parts_out(l, b):
                for n, (rows, pick) in enumerate(((q_rows[l], Q_PART), (k_rows[l], K_PART))):
                    for h in (0, 1):
                        hold(stack_in[l][h], 64 * b)
                    hold(part2[2 * l + n], b + 1)
                    for j0, j1 in ((0, 3), (3, 5), (5, 6)):
                        step = pick[j0 + 1] - pick[j0] if j1 - j0 > 1 else 0
                        sp.dma_start(rows[:, j0:j1, :],
                                     bass.AP(qp[l][n][:, :, :].tensor, pick[j0] * SEQ,
                                             [[PARTS * SEQ, 128], [step * SEQ, j1 - j0], [1, SEQ]])
                                     ).then_inc(rows_out[l][n], 16)

            def stack_half(l, half, b):
                for n in (0, 1):
                    hold(rows_out[l][n], 48 * (b + 1))
                if not isinstance(b, int) or b > 0:
                    hold(scores, UNITS * attends_before(l, b - 1) + 32 * (half + 1))
                for rows, stacks in ((q_rows[l], (q_stack[l], q_stack[l])), (k_rows[l], k_stack[l])):
                    for e in (0, 1):
                        src = bass.AP(rows.tensor, (64 * e + 32 * half) * TERMS * SEQ,
                                      [[SEQ, KROWS], [HD * TERMS * SEQ, 4], [1, SEQ]])
                        sp.dma_start(stacks[e][KROWS * e:KROWS * e + KROWS, 4 * half:4 * half + 4, :], src
                                     ).then_inc(stack_in[l][half], 16)

            def max_rows(l, quarter, b):
                hold(read[f"m{l}"], 4 * b + quarter + 1)
                sp.dma_start(q_stack[l][QROWS:QROWS + 2 * MROWS, 2 * quarter:2 * quarter + 2, :],
                             m_parts[l][quarter % 2][:, :]).then_inc(m_in[l][quarter], 16)

            def den_lines(l, b):
                hold(o_saved, 2 * attends_before(l, b) + 2)
                sp.dma_start(den[l][:, :],
                             bass.AP(o_raw[l][:, :, :].tensor, 8 * 2 * SEQ, [[16 * 2 * SEQ, 8], [64, 16], [1, 64]])
                             ).then_inc(den_in[l], 16)

            def rden_lines(l, b):
                hold(rden_ready[l], b + 1)
                hold(rden_in[l], 16 * b)
                sp.dma_start(bass.AP(rden_rows[l].tensor, 0, [[64, 128], [1, 64]]), rden[l][:, :]
                             ).then_inc(rden_out[l], 16)
                hold(rden_out[l], 16 * (b + 1))
                hold(att_ready[l], b)
                sp.dma_start(rden_all[l][:, :, :].rearrange("p c s -> p (c s)"),
                             bass.AP(rden_rows[l].tensor, 0, [[2 * SEQ, 8], [0, 16], [1, 2 * SEQ]])
                             ).then_inc(rden_in[l], 16)

            def slot(kind, i, at):
                have = parts_of(kind, at)
                if kind == "X":
                    if "P0" in have:
                        load_x(i + 1)
                    if "E" in have:
                        den_lines(1, i - 2)
                    if "MXt" in have:
                        max_rows(0, 1, i)
                    if "E" in have:
                        rden_lines(1, i - 2)
                    if "MXt" in have:
                        max_rows(0, 2, i)
                    if "M2" in have:
                        parts_out(1, i - 1)
                        stack_half(1, 0, i - 1)
                        stack_half(1, 1, i - 1)
                    if "MXt" in have:
                        max_rows(0, 3, i)
                    if "M2" in have:
                        hold(read["dn"], i)
                        if "E" in have:
                            hold(read["pr1"], i - 1)
                        sp.dma_start(res[1][:, :, :], x2[:, :, :]).then_inc(res_copied[1], 16)
                    if "P0" in have:
                        parts_out(0, i + 1)
                        stack_half(0, 0, i + 1)
                    if "MXh" in have:
                        max_rows(1, 0, i - 1)
                    if "E" in have:
                        hold(read["out"], i - 1)
                        dst = out_dram[at - 2:at - 1] if isinstance(i, int) else out_dram[bass.ds(i - 2, 1)]
                        sp.dma_start(dst.rearrange("a (t p) d -> p (a t) d", p=128), x3[:, :, :]).then_inc(stored, 16)
                    if "P0" in have:
                        stack_half(0, 1, i + 1)
                else:
                    if at == -1:
                        parts_out(0, 0)
                        hold(k_ones, 4)
                        stack_half(0, 0, 0)
                        stack_half(0, 1, 0)
                        max_rows(0, 0, 0)
                        return
                    if "MXt" in have:
                        max_rows(1, 1, i - 1)
                    if "M1" in have:
                        den_lines(0, i)
                        rden_lines(0, i)
                    if "MXt" in have:
                        max_rows(1, 2, i - 1)
                    if "V0" in have:
                        hold(read["pr0"], i + 1)
                        hold(x_loaded, 16 * (i + 2))
                        sp.dma_start(res[0][:, :, :], x_in[:, :, :]).then_inc(res_copied[0], 16)
                    if "MXt" in have:
                        max_rows(1, 3, i - 1)
                    if "MXh" in have:
                        max_rows(0, 0, i + 1)

            walk(sp, slot)
            hold(stored, 16 * BATCH)

        @block.gpsimd
        def _(pool):
            pool.memset(ident[:, :], 0.0).then_inc(ident_zero, 1)
            pool.wait_ge(ident_zero, 1)
            pool.affine_select(out=ident[:, :], in_=ident[:, :], compare_op=ALU.not_equal, fill=1.0, base=0,
                               pattern=[[-1, 128]], channel_multiplier=1).then_inc(ident_ready, 1)
            pool.memset(half_neg[:, :], -0.5)
            pool.memset(mid_bias[:, EXPERTS:], 0.0)
            flat = [t[:, :, :].rearrange("p a b -> p (a b)") for t in (*k_stack[0], *k_stack[1], *q_stack)]
            for t in flat:
                pool.memset(t.bitcast(F32), 0.0).then_inc(k_zeros, 1)

            def norm_factors(k, b):
                pool.wait_ge(var_ready[k], b + 1)
                pool.tensor_tensor(rstd[k][:, :], vpe[k][:, :], half_neg[:, :], ALU.pow).then_inc(rstd_ready[k], 1)
                pool.wait_ge(rstd_ready[k], b + 1)
                pool.tensor_tensor(shift[k][:, :], neg_mean[k][:, :], rstd[k][:, :], ALU.mult).then_inc(shift_ready[k], 1)

            def residual1(l, n, b):
                pool.wait_ge(read[(("q0", "k0"), ("qt", "kt"))[l][n]], b + 1)
                pool.tensor_tensor(qf[l][n][:, :], qf[l][n][:, :], qp[l][n][:, 0, :], ALU.subtract
                                   ).then_inc(resid1[2 * l + n], 1)

            def residual2(l, n, b):
                pool.wait_ge(part1[2 * l + n], b + 1)
                pool.tensor_tensor(qp[l][n][:, 2, :], qf[l][n][:, :], qp[l][n][:, 1, :], ALU.subtract
                                   ).then_inc(part2[2 * l + n], 1)

            def normalise(l, b):
                pool.wait_ge(rden_in[l], 16 * (b + 1))
                pool.tensor_tensor(o_raw[l][:, :, :], o_raw[l][:, :, :], rden_all[l][:, :, :], ALU.mult
                                   ).then_inc(att_ready[l], 1)

            def scale_qk(n, b):
                if n == 0:
                    pool.wait_ge(newton, N_NEWTON * (b + 1))
                x = qk1[:, :, D * n:D * n + D].rearrange("p t (h e) -> p t h e", e=HD)
                inv = nw_y[:, :].rearrange("p (t n h) -> p t n h", t=TT, n=2)[:, :, n, :]
                for t in range(TT):
                    last = pool.tensor_tensor(x[:, t, :, :], x[:, t, :, :], wide(inv[:, t, :, None], 2, HD), ALU.mult)
                last.then_inc(qk_normed[n], 1)

            def mix(b):
                pool.wait_ge(gate_ready, b + 1)
                need(pool, read["ct"], b)
                for t in range(TT):
                    last = pool.tensor_tensor(coef[:, t, :].rearrange("p (e r) -> p e r", r=RANK),
                                              wide(gating[:, t, :, None], 2, RANK),
                                              wide(rm[:, t, None, EXPERTS:], 1, EXPERTS), ALU.mult)
                last.then_inc(coef_ready, 1)

            def slot(kind, i, at):
                have = parts_of(kind, at)
                if kind == "X":
                    if "M2" in have:
                        scale_qk(0, i - 1)
                        scale_qk(1, i - 1)
                    if "P0" in have:
                        norm_factors(0, i + 1)
                    if "M2" in have:
                        for n in (0, 1):
                            residual1(1, n, i - 1)
                            residual2(1, n, i - 1)
                    if "E" in have:
                        normalise(1, i - 2)
                        norm_factors(3, i - 2)
                    if "P0" in have:
                        for n in (0, 1):
                            residual1(0, n, i + 1)
                            residual2(0, n, i + 1)
                    if "E" in have:
                        mix(i - 2)
                else:
                    if at == -1:
                        norm_factors(0, 0)
                        for n in (0, 1):
                            residual1(0, n, 0)
                            residual2(0, n, 0)
                    if "M1" in have:
                        normalise(0, i)
                        norm_factors(1, i)
                        norm_factors(2, i)

            walk(pool, slot)

        @block.scalar
        def _(act):
            def copy(dst, src):
                return act.activation(dst, src, ACT.Copy)

            act.wait_ge(w_turned, 1)
            for l in (0, 1):
                copy(wo[l][:, :, :], ps[:, 0, 256 * l:256 * l + 256].rearrange("p (c n) -> p c n", c=2))
            copy(w_gate[:, :, :], ps[:, 1, 0:384].rearrange("p (c n) -> p c n", c=3))
            copy(w_up[:, :, :], ps[:, 2, 0:384].rearrange("p (c n) -> p c n", c=3))
            copy(w_down[:, :, :], ps[:, 3, 0:384].rearrange("p (c n) -> p c n", c=3))
            copy(wqkv[:, :], ps[:, 4, 0:384])
            copy(w_base[:, :], ps[:, 5, 0:128])
            copy(w_mid[:, 0:EXPERTS], ps[:, 5, 128:136]).then_inc(w_ready, 1)

            def exp_unit(l, u, b):
                a = attends_before(l, b)
                act.wait_ge(scores, UNITS * a + u + 1)
                if u % 4 == 0 and not (isinstance(a, int) and a == 0 and u < RING):
                    act.wait_ge(pv, 16 * a + (u - RING) // 4 + 1)
                act.activation(probs[:, u % RING, :], ps[:, bank_of(l, u), :], ACT.Exp).then_inc(exps, 1)

            def apply_norm(k, x, b):
                act.wait_ge(shift_ready[k], b + 1)
                for t in range(TT):
                    last = act.activation(xn[k][:, t, :], x[:, t, :], ACT.Identity, bias=shift[k][:, t:t + 1],
                                          scale=rstd[k][:, t:t + 1])
                last.then_inc(xn_ready[k], 1)

            def save_out(l, half, b):
                act.wait_ge(pv, 16 * attends_before(l, b) + 8 * (half + 1))
                need(act, read[("pr0", "pr1")[l]], b)
                copy(o_raw[l][:, half, :], acc).then_inc(o_saved, 1)

            def take(name, dst, b):
                act.wait_ge(written[name], b + 1)
                copy(dst, gen).then_inc(read[name], 1)

            def take_qk(l, n, b):
                name = (("q0", "k0"), ("qt", "kt"))[l][n]
                act.wait_ge(written[name], b + 1)
                need(act, rows_out[l][n], 48 * b)
                if l == 0:
                    bias = (bq_scaled[:, 0:1], qk_bias[:, 1:2])[n]
                    kw = dict(scale=(QK_SCALE, 1.0)[n], bias=bias)
                else:
                    kw = dict(scale=(qn_scaled[:, 0:1], norm_w[:, 1:2])[n])
                act.activation(qf[l][n][:, :], gen, ACT.Identity, **kw)
                act.activation(qp[l][n][:, 0, :], gen, ACT.Identity, **kw).then_inc(read[name], 1)

            def take_part1(l, n, b):
                act.wait_ge(resid1[2 * l + n], b + 1)
                copy(qp[l][n][:, 1, :], qf[l][n][:, :]).then_inc(part1[2 * l + n], 1)

            def take_max(l, quarter, b):
                act.wait_ge(written[f"m{l}"], 4 * b + quarter + 1)
                if quarter < 2:
                    need(act, m_in[l][quarter + 2], 16 * b)
                else:
                    act.wait_ge(m_in[l][quarter - 2], 16 * (b + 1))
                copy(m_parts[l][quarter % 2][:, :], gen[0:32, 0:128]).then_inc(read[f"m{l}"], 1)

            def gate_tanh(c, b):
                act.wait_ge(written[f"g{c}"], b + 1)
                act.activation(th[:, :], gen, ACT.Tanh, scale=0.5).then_inc(tanh_done, 1)

            def square(half, b):
                act.wait_ge(read[("qka", "qkb")[half]], b + 1)
                act.activation(sq[:, 2 * half:2 * half + 2, :], qk1[:, 2 * half:2 * half + 2, :], ACT.Square
                               ).then_inc(squared, 1)

            def gate_exp(b):
                act.wait_ge(moe, 3 * (b + 1) + 1 * b)
                act.activation(lexp[:, :, :], lsh[:, :, :], ACT.Exp).then_inc(l_exp, 1)

            def take_coef(b):
                act.wait_ge(written["ct"], b + 1)
                need(act, read["out"], b)
                copy(coef_t[0:EXPERTS * RANK, :], gen[0:EXPERTS * RANK, :]).then_inc(read["ct"], 1)

            def slot(kind, i, at):
                have = parts_of(kind, at)
                if at == -1:
                    act.wait_ge(w_placed, 1)
                    apply_norm(0, x_in, 0)
                    take("xt0", xnt[0][:, :], 0)
                    for n in (0, 1):
                        take_qk(0, n, 0)
                        take_part1(0, n, 0)
                    take_max(0, 0, 0)
                    return
                for s in range(STEPS):
                    if "A" in have:
                        for u in (2 * s, 2 * s + 1):
                            exp_unit(0 if kind == "X" else 1, u, i if kind == "X" else i - 1)
                    tail, head = ((0, i), (1, i - 1)) if kind == "X" else ((1, i - 1), (0, i + 1))
                    if s in M_TAIL and "MXt" in have:
                        take_max(tail[0], 1 + M_TAIL.index(s), tail[1])
                    if s == M_HEAD and "MXh" in have:
                        take_max(head[0], 0, head[1])
                    if kind == "X":
                        if s == 2 and "At" in have:
                            save_out(1, 1, i - 2)
                        if s == 18 and "A" in have:
                            save_out(0, 0, i)
                        if "M2" in have:
                            if s in (7, 8):
                                take_qk(1, s - 7, i - 1)
                            if s in (9, 12):
                                take_part1(1, (s - 9) // 3, i - 1)
                        if "P0" in have:
                            if s == 15:
                                apply_norm(0, x_in, i + 1)
                            if s == 17:
                                take("xt0", xnt[0][:, :], i + 1)
                            if s in (19, 21):
                                take_qk(0, (s - 19) // 2, i + 1)
                        if "E" in have and s == 20:
                            apply_norm(3, x3, i - 2)
                        if "E" in have and s == 22:
                            take("xt3", xnt[3][:, :], i - 2)
                        if "P0" in have and s in (23, 25):
                            take_part1(0, (s - 23) // 2, i + 1)
                        if "E" in have:
                            if s == 25:
                                gate_exp(i - 2)
                            if s == 28:
                                take_coef(i - 2)
                    else:
                        if s == 2 and "At" in have:
                            save_out(0, 1, i)
                        if s == 18 and "A" in have:
                            save_out(1, 0, i - 1)
                        if "M1" in have:
                            if s == 12:
                                apply_norm(1, x1, i)
                            if s == 13:
                                take("xt1", xnt[1][:, :], i)
                            if s in (14, 16, 20):
                                gate_tanh((14, 16, 20).index(s), i)
                            if s == 26:
                                apply_norm(2, x2, i)
                            if s == 27:
                                take("xt2", xnt[2][:, :], i)
                            if s in (29, 30):
                                square(s - 29, i)

            walk(act, slot)

        @block.vector
        def _(dve):
            dve.memset(coef_t[64:65, :], 1.0)
            dve.wait_ge(w_loaded, 16 * 24)
            for l in (0, 1):
                dve.memset(v_aug[l][:, :, :, :].rearrange("p a b c -> p (a b c)"), 0.0)
                dve.memset(wo_perm[l], 0.0).then_inc(v_zeros, 1)
            dve.wait_ge(v_zeros, 2)
            for l in (0, 1):
                for c in (0, 1):
                    for s in (0, 1):
                        dst = wo_perm[l][:, 128 * c:128 * c + 128].rearrange("n (pp e s d) -> n e pp s d", pp=2, e=2, s=2)
                        src = wo_nat[l].rearrange("n (e c s pp d) -> n e c s pp d", e=2, c=2, s=2, pp=2)
                        dve.tensor_copy(dst[:, :, :, s, 0:HD], src[:, :, c, s, :, :])
                dve.tensor_copy(wo_perm[l][:, HD:HD + 1], bo_col[l])
                for s in (0, 1):
                    dve.memset(v_aug[l][:, :, :, :].rearrange("p t (r s pp) m -> p (t r) s pp m", s=2, pp=2)
                               [:, :, s, :, 16 * s + HD:16 * s + HD + 1], 1.0)
            for n in range(3):
                dve.tensor_scalar(flt_w[n], int_w[n], DEQUANT, (1.0, 1.0, 0.5)[n], ALU.mult, ALU.mult)
            dve.tensor_scalar(bq_scaled[:, :], qk_bias[:, 0:1], QK_SCALE, None, ALU.mult)
            dve.tensor_scalar(qn_scaled[:, :], norm_w[:, 0:1], QK_SCALE, None, ALU.mult)
            dve.tensor_scalar(w_lora[0:64, :], lora_nat, LORA_SCALE, None, ALU.mult).then_inc(w_placed, 1)

            dve.wait_ge(k_zeros, 6)
            for l in (0, 1):
                k0, k1 = (t[:, :, :].rearrange("p a b -> p (a b)") for t in k_stack[l])
                dve.memset(k0[QROWS:QROWS + MROWS, :], 1.0).then_inc(k_ones, 1)
                dve.memset(k1[QROWS:QROWS + 2 * MROWS, :], 1.0).then_inc(k_both, 1)
                dve.wait_ge(k_both, l + 1)
                dve.memset(k1[QROWS:QROWS + MROWS, :], 0.0).then_inc(k_ones, 1)

            def stats(k, x, b):
                need(dve, xn_ready[k], b)
                for t in range(TT):
                    last = dve.bn_stats(bn[k][:, t, :], x[:, t, :])
                last.then_inc(bn_done[k], 1)

            def moments(k, b):
                wait_apart(dve, bn_done[k], b + 1, passed)
                for t in range(TT):
                    last = dve.bn_aggr(mv[k][:, t, :], bn[k][:, t, :])
                last.then_inc(mv_done[k], 1)
                dve.wait_ge(mv_done[k], b + 1)
                dve.tensor_scalar(neg_mean[k][:, :], mv[k][:, :, 0], -1.0, None, ALU.mult)
                dve.tensor_scalar(vpe[k][:, :], mv[k][:, :, 1], LN_EPS, None, ALU.add).then_inc(var_ready[k], 1)


            def max_step(l, n, b):
                base = 2 * STEPS * maxima_before(l, b) + 2 * n
                pair, st = n // 4, n % 4
                for e in (0, 1):
                    dve.wait_ge(max_scores, base + e + 1)
                    col = 16 * e + 4 * (pair % 2) + st
                    bank = SCORE_BANKS + bank_of(l, 2 * n + e)
                    dve.tensor_reduce(neg_max[l][:, pair // 2, col:col + 1], ps[:, bank, :], AX.X, ALU.max,
                                      negate=True).then_inc(max_taken, 1)

            def split_max(l, quarter, b):
                done = 4 * maxima_before(l, b) + quarter + 1
                dve.wait_ge(max_taken, 16 * done)
                parts = neg_max[l][:, quarter, :].rearrange("p (e j c) -> p e j c", e=2, j=2)
                high = neg_high[l][:, quarter, :].rearrange("p (e c) -> p e c", e=2)
                dve.tensor_copy(high, parts[:, :, 0, :]).then_inc(high_done, 1)
                dve.wait_ge(high_done, done)
                dve.tensor_tensor(parts[:, :, 1, :], parts[:, :, 0, :], high, ALU.subtract).then_inc(low_done[l], 1)

            def take_v(l, b):
                name = ("v0", "v1")[l]
                dve.wait_ge(written[name], b + 1)
                src = gen.rearrange("p (r s m) -> p r s m", s=2, m=2 * HD)
                bias = v_bias[l][:, :].rearrange("p (r s m) -> p r s m", s=2, m=2 * HD)
                dst = v_aug[l][:, :, :, :].rearrange("p t (r s pp) m -> p (t r) s pp m", s=2, pp=2)
                for t in range(TT):
                    for s in (0, 1):
                        last = dve.tensor_tensor(
                            dst[:, 4 * t:4 * t + 4, s, :, 16 * s:16 * s + HD],
                            src[:, 4 * t:4 * t + 4, s, :].rearrange("p r (pp d) -> p r pp d", d=HD),
                            bias[:, :, s, :].rearrange("p r (pp d) -> p r pp d", d=HD), ALU.add)
                last.then_inc(read[name], 1)

            def invert_den(l, b):
                dve.wait_ge(den_in[l], 16 * (b + 1))
                need(dve, rden_out[l], 16 * b)
                dve.reciprocal(rden[l][:, :], den[l][:, :]).then_inc(rden_ready[l], 1)

            def add_into(name, dst, other, b):
                dve.wait_ge(written[name], b + 1)
                dve.tensor_tensor(dst[:, :, :], gen4, other[:, :, :], ALU.add).then_inc(read[name], 1)

            def project_add(l, dst, b):
                dve.wait_ge(res_copied[l], 16 * (b + 1))
                if l == 1:
                    need(dve, stored, 16 * b)
                add_into(("pr0", "pr1")[l], dst, res[l], b)

            def gate_mul(c, b):
                dve.wait_ge(tanh_done, NH * b + c + 1)
                dve.scalar_tensor_tensor(out=gs[:, :], in0=th[:, :], scalar=1.0, in1=gen, op0=ALU.add,
                                         op1=ALU.mult).then_inc(read[f"g{c}"], 1)

            def up_mul(c, b):
                dve.wait_ge(written[f"u{c}"], b + 1)
                dve.tensor_tensor(ht[:, c, :], gen, gs[:, :], ALU.mult).then_inc(read[f"u{c}"], 1)

            def down_add(b):
                need(dve, res_copied[1], 16 * b)
                add_into("dn", x2, x1, b)

            def take_qk1(half, b):
                name = ("qka", "qkb")[half]
                dve.wait_ge(written[name], b + 1)
                for t in (0, 1):
                    last = dve.tensor_tensor(qk1[:, 2 * half + t, :], gen[:, 256 * t:256 * t + 256], qk1_bias[:, :], ALU.add)
                last.then_inc(read[name], 1)

            def inverse_rms(first, count, b):
                for n in range(first, first + count):
                    if n < 2:
                        dve.wait_ge(squared, 2 * b + n + 1)
                        op = dve.tensor_reduce(ms[:, 64 * n:64 * n + 64],
                                               sq[:, 2 * n:2 * n + 2, :].rearrange("p t (g e) -> p (t g) e", e=HD),
                                               AX.X, ALU.add)
                    else:
                        dve.wait_ge(newton, N_NEWTON * b + n)
                        if n == 2:
                            op = dve.tensor_scalar(ms[:, :], ms[:, :], 1.0 / HD, RMS_EPS, ALU.mult, ALU.add)
                        elif n == 3:
                            op = dve.tensor_scalar(nw_t[:, :].bitcast(I32), ms[:, :].bitcast(I32), 1, None,
                                                   ALU.logical_shift_right)
                        elif n == 4:
                            op = dve.tensor_scalar(nw_y[:, :].bitcast(I32), nw_t[:, :].bitcast(I32), -1.0,
                                                   float(0x5f3759df), ALU.mult, ALU.add)
                        elif n % 3 == 2:
                            op = dve.tensor_tensor(nw_t[:, :], nw_y[:, :], nw_y[:, :], ALU.mult)
                        elif n % 3 == 0:
                            op = dve.scalar_tensor_tensor(out=nw_u[:, :], in0=nw_t[:, :], scalar=-0.5, in1=ms[:, :],
                                                          op0=ALU.mult, op1=ALU.mult)
                        else:
                            op = dve.scalar_tensor_tensor(out=nw_y[:, :], in0=nw_u[:, :], scalar=1.5, in1=nw_y[:, :],
                                                          op0=ALU.add, op1=ALU.mult)
                    op.then_inc(newton, 1)

            def route(b):
                dve.wait_ge(written["rt"], b + 1)
                at = 4 * b
                dve.tensor_tensor(rm[:, :, :], gen[:, 0:TT * 16].rearrange("p (t n) -> p t n", t=TT),
                                  wide(mid_bias[:, None, :], 1, TT), ALU.add).then_inc(read["rt"], 1)
                dve.wait_ge(read["rt"], b + 1)
                dve.tensor_reduce(lmax[:, :], rm[:, :, 0:EXPERTS], AX.X, ALU.max).then_inc(moe, 2)
                dve.wait_ge(moe, at + 2)
                dve.tensor_tensor(lsh[:, :, :], rm[:, :, 0:EXPERTS], wide(lmax[:, :, None], 2, EXPERTS),
                                  ALU.subtract).then_inc(moe, 1)

            def gates(b):
                dve.wait_ge(l_exp, b + 1)
                dve.tensor_reduce(lsum[:, :], lexp[:, :, :], AX.X, ALU.add).then_inc(moe, 1)
                dve.wait_ge(moe, 4 * b + 4)
                dve.reciprocal(lrec[:, :], lsum[:, :]).then_inc(m_rec, 1)
                dve.wait_ge(m_rec, b + 1)
                dve.tensor_tensor(gating[:, :, :], lexp[:, :, :], wide(lrec[:, :, None], 2, EXPERTS), ALU.mult
                                  ).then_inc(gate_ready, 1)

            def finish(b):
                add_into("out", x3, x3, b)

            def slot(kind, i, at):
                have = parts_of(kind, at)
                if at == -1:
                    dve.wait_ge(x_loaded, 16)
                    stats(0, x_in, 0)
                    moments(0, 0)
                tail, head = ((0, i), (1, i - 1)) if kind == "X" else ((1, i - 1), (0, i + 1))
                for s in range(STEPS):
                    if at == -1 and s == 6:
                        take_v(0, 0)
                    if s < LEAD and "MXt" in have:
                        n = s + STEPS - LEAD
                        max_step(tail[0], n, tail[1])
                        if n % 8 == 7:
                            split_max(tail[0], n // 8, tail[1])
                    if s >= LEAD and "MXh" in have:
                        n = s - LEAD
                        max_step(head[0], n, head[1])
                        if n % 8 == 7:
                            split_max(head[0], n // 8, head[1])
                    if kind == "X":
                        if "M2" in have:
                            if s < 6:
                                inverse_rms(2 + 2 * s, 2, i - 1)
                            if s == 6:
                                take_v(1, i - 1)
                        if "P0" in have:
                            if s == 7:
                                dve.wait_ge(x_loaded, 16 * (i + 2))
                                stats(0, x_in, i + 1)
                            if s == 8:
                                moments(0, i + 1)
                        if "E" in have:
                            if s == 4:
                                invert_den(1, i - 2)
                            if s == 16:
                                project_add(1, x3, i - 2)
                            if s == 17:
                                dve.wait_ge(read["pr1"], i - 1)
                                stats(3, x3, i - 2)
                            if s == 18:
                                moments(3, i - 2)
                            if s == 24:
                                route(i - 2)
                            if s == 26:
                                gates(i - 2)
                            if s == 30:
                                finish(i - 2)
                    else:
                        if s == 5 and "V0" in have and at >= 0:
                            take_v(0, i + 1)
                        if "M1" in have:
                            if s == 4:
                                invert_den(0, i)
                            if s == 10:
                                project_add(0, x1, i)
                            if s == 10:
                                dve.wait_ge(read["pr0"], i + 1)
                                stats(1, x1, i)
                            if s == 11:
                                moments(1, i)
                            if s in (14, 16, 20):
                                gate_mul((14, 16, 20).index(s), i)
                            if s in (15, 17, 21):
                                up_mul((15, 17, 21).index(s), i)
                            if s == 23:
                                down_add(i)
                            if s == 24:
                                dve.wait_ge(read["dn"], i + 1)
                                stats(2, x2, i)
                            if s == 25:
                                moments(2, i)
                            if s in (28, 29):
                                take_qk1(s - 28, i)
                            if s in (30, 31):
                                inverse_rms(s - 30, 1, i)

            walk(dve, slot)

        @block.tensor
        def _(pe):
            def turn(dst, src, n=128):
                return pe.transpose(dst, src, ident[0:n, 0:n])

            pe.wait_ge(ident_ready, 1)
            pe.wait_ge(w_placed, 1)
            for l in (0, 1):
                for c in (0, 1):
                    turn(ps[:, 0, 256 * l + 128 * c:256 * l + 128 * c + 128], wo_perm[l][:, 128 * c:128 * c + 128])
            for n, w in enumerate((flt_w[0], flt_w[1], flt_w[2], wqkv_nat)):
                for c in range(3):
                    turn(ps[:, 1 + n, 128 * c:128 * c + 128], w[:, 128 * c:128 * c + 128])
            turn(ps[:, 5, 0:128], base_nat)
            turn(ps[:, 5, 128:128 + EXPERTS], router_nat, EXPERTS).then_inc(w_turned, 1)
            pe.wait_ge(w_ready, 1)
            pe.wait_ge(k_ones, 4)

            def max_score(l, n, e, b):
                base = 2 * STEPS * maxima_before(l, b)
                if e == 0 and n % 16 == 0:
                    pe.wait_ge(stack_in[l][n // 16], 64 * (b + 1))
                need(pe, max_taken, free_at(l, 2 * n + e, b, base))
                tok, pair = 128 * (n % 4), n // 4
                pe.matmul(ps[:, SCORE_BANKS + bank_of(l, 2 * n + e), :], q_stack[l][0:QROWS, pair, tok:tok + 128],
                          k_stack[l][e][0:QROWS, pair, :], start=True, stop=True).then_inc(max_scores, 1)

            def attend_score(l, u, b):
                group, kt, pp, e = u // 16, (u % 16) // 4, (u % 4) // 2, u % 2
                if u % 16 == 0:
                    pe.wait_ge(m_in[l][u // 16], 16 * (b + 1))
                need(pe, exps, free_at(l, u, b, UNITS * attends_before(l, b)))
                tok, pair = 128 * kt, 2 * group + pp
                pe.matmul(ps[:, bank_of(l, u), :], k_stack[l][e][:, pair, tok:tok + 128],
                          q_stack[l][:, pair, :], start=True, stop=True).then_inc(scores, 1)

            def attend_pv(l, u, b):
                group, kt = u // 16, (u % 16) // 4
                c, s = group // 2, group % 2
                a = attends_before(l, b)
                if u == 0:
                    pe.wait_ge(read[("v0", "v1")[l]], b + 1)
                if u % 32 == 0:
                    need(pe, o_saved, 2 * a + c)
                pe.wait_ge(exps, UNITS * a + u + 4)
                for j in range(4):
                    pp, e = j // 2, j % 2
                    last = pe.matmul(acc[32 * j:32 * j + 32, :], v_aug[l][:, kt, 8 * e + 2 * group + pp, :],
                                     probs[:, (u + j) % RING, :], start=(s == 0 and kt == 0),
                                     stop=(s == 1 and kt == TT - 1))
                last.then_inc(pv, 1)

            def turn_norm(k, b):
                pe.wait_ge(xn_ready[k], b + 1)
                for t in range(TT):
                    last = turn(gen[:, 128 * t:128 * t + 128], xn[k][:, t, :])
                return last

            def by_token(dst, xt, w, more=None):
                for t in range(TT):
                    last = pe.matmul(dst[:, t, :], xt[:, 128 * t:128 * t + 128], w, start=True, stop=more is None)
                    if more is not None:
                        last = pe.matmul(dst[:, t, :], more[0][:, 128 * t:128 * t + 128], more[1], start=False, stop=True)
                return last

            def project(l, b):
                pe.wait_ge(att_ready[l], b + 1)
                for t in range(TT):
                    for c in (0, 1):
                        last = pe.matmul(gen4[:, t, :], o_raw[l][:, c, 128 * t:128 * t + 128], wo[l][:, c, :],
                                         start=c == 0, stop=c == 1)
                return last

            def piece(name, i, at, kind, b):
                before = piece_before(kind, at, name)
                if before is not None:
                    pe.wait_ge(read[sem_name(before[0])], count(before[0], i + before[1]))
                if name in ("xt0", "xt1", "xt2", "xt3"):
                    last = turn_norm(int(name[2]), b)
                elif name in ("q0", "k0"):
                    pe.wait_ge(read["xt0"], b + 1)
                    last = pe.matmul(gen, (wq if name == "q0" else wk)[:, :], xnt[0][:, :], start=True, stop=True)
                elif name == "v0":
                    pe.wait_ge(read["xt0"], b + 1)
                    last = by_token(gen4, xnt[0], wv[:, :])
                elif name == "v1":
                    last = by_token(gen4, xnt[2], wqkv[:, 256:384])
                elif name[0] == "m":
                    l, quarter = int(name[1]), int(name[2])
                    pe.wait_ge(low_done[l], 4 * b + quarter + 1)
                    last = turn(gen[0:32, 0:128], neg_max[l][:, quarter, :])
                elif name in ("pr0", "pr1"):
                    last = project(int(name[2]), b)
                elif name[0] in "gu":
                    pe.wait_ge(read["xt1"], b + 1)
                    w = w_gate if name[0] == "g" else w_up
                    last = pe.matmul(gen, w[:, int(name[1]), :], xnt[1][:, :], start=True, stop=True)
                elif name == "dn":
                    for t in range(TT):
                        for c in range(NH):
                            last = pe.matmul(gen4[:, t, :], ht[:, c, 128 * t:128 * t + 128], w_down[:, c, :],
                                             start=c == 0, stop=c == NH - 1)
                elif name in ("qka", "qkb"):
                    pe.wait_ge(read["xt2"], b + 1)
                    half = int(name == "qkb")
                    for t in (0, 1):
                        tok = 128 * (2 * half + t)
                        last = pe.matmul(gen[:, 256 * t:256 * t + 256], xnt[2][:, tok:tok + 128], wqkv[:, 0:256],
                                         start=True, stop=True)
                elif name in ("qt", "kt"):
                    pe.wait_ge(qk_normed[int(name == "kt")], b + 1)
                    for t in range(TT):
                        c = 128 * (name == "kt")
                        last = turn(gen[:, 128 * t:128 * t + 128], qk1[:, t, c:c + 128])
                elif name == "rt":
                    pe.wait_ge(read["xt3"], b + 1)
                    last = by_token(gen[:, 0:TT * 16].rearrange("p (t n) -> p t n", t=TT), xnt[3], w_mid[:, :])
                elif name == "ct":
                    wait_apart(pe, coef_ready, b + 1, passed)
                    for t in range(TT):
                        last = turn(gen[0:64, 128 * t:128 * t + 128], coef[:, t, :])
                elif name == "out":
                    last = by_token(gen4, xnt[3], w_base[:, :], more=(coef_t, w_lora[:, :]))
                last.then_inc(written[sem_name(name)], 1)

            def slot(kind, i, at):
                have = parts_of(kind, at)
                pieces = slot_pieces(kind, at)
                if at == -1:
                    for name in ("xt0", "q0", "k0", "v0"):
                        if name == "xt0":
                            last = turn_norm(0, 0)
                        elif name == "v0":
                            pe.wait_ge(read["k0"], 1)
                            last = by_token(gen4, xnt[0], wv[:, :])
                        else:
                            pe.wait_ge(read["xt0" if name == "q0" else "q0"], 1)
                            last = pe.matmul(gen, (wq if name == "q0" else wk)[:, :], xnt[0][:, :], start=True, stop=True)
                        last.then_inc(written[name], 1)
                    pieces = [p for p in pieces if p[1] != "v0"]
                tail, head = ((0, i), (1, i - 1)) if kind == "X" else ((1, i - 1), (0, i + 1))
                now, past = ((0, i), (1, i - 2)) if kind == "X" else ((1, i - 1), (0, i))
                for s in range(STEPS):
                    mx = None
                    if s < LEAD and "MXt" in have:
                        mx = (tail[0], s + STEPS - LEAD, tail[1])
                    if s >= LEAD and "MXh" in have:
                        mx = (head[0], s - LEAD, head[1])
                    for e in (0, 1):
                        if "A" in have:
                            attend_score(now[0], 2 * s + e, now[1])
                        if mx:
                            max_score(mx[0], mx[1], e, mx[2])
                    if s == 1 and "At" in have:
                        attend_pv(past[0], UNITS - 4, past[1])
                    if s % 2 and s > 1 and "A" in have:
                        attend_pv(now[0], 2 * s - 6, now[1])
                    for at_step, name in pieces:
                        if at_step == s:
                            piece(name, i, at, kind, i + PIECE[name][0])

            walk(pe, slot)


NAMES = ["L0_attn_x", "L0_attn_wq", "L0_attn_bq", "L0_attn_wk", "L0_attn_bk", "L0_attn_wv", "L0_attn_bv",
         "L0_attn_wo", "L0_attn_bo", "L0_ffn_w_gate", "L0_ffn_w_up", "L0_ffn_w_down", "L1_attn_Wqkv",
         "L1_attn_bqkv", "L1_attn_Wproj", "L1_attn_bproj", "L1_attn_qn_w", "L1_attn_kn_w", "L1_ffn_base_w",
         "L1_ffn_base_b", "L1_ffn_lora_A", "L1_ffn_lora_B", "L1_ffn_router_w", "L1_ffn_router_b"]


def kernel(**inputs):
    import numpy as _np
    import concourse.bacc as _bacc
    from concourse import mybir as _mybir
    from concourse.bass_utils import run_bass_kernel_spmd as _run

    nc = _bacc.Bacc("TRN2", target_bir_lowering=False, num_devices=1)
    arrays, tensors = {}, {}
    for name in NAMES:
        a = _np.ascontiguousarray(inputs[name])
        arrays[f"in_{name}"] = a
        tensors[name] = nc.dram_tensor(f"in_{name}", a.shape, _mybir.dt.from_np(a.dtype), kind="ExternalInput").ap()
    out = nc.dram_tensor("out_x", (BATCH, SEQ, D), F32, kind="ExternalOutput").ap()
    build(nc, tensors, out)
    r = _run(nc, [arrays], core_ids=[0])
    return r.results[0]["out_x"]
```

```python
import numpy as np
import concourse.bass as bass
from concourse import mybir
from contextlib import ExitStack

F32 = mybir.dt.float32
BF16 = mybir.dt.bfloat16
I32 = mybir.dt.int32
ALU = mybir.AluOpType
ACT = mybir.ActivationFunctionType
AX = mybir.AxisListType

BATCH, SEQ, D = 16, 512, 128
HEADS, HD = 16, 8
TT = SEQ // 128
NH = 3
EXPERTS, RANK = 8, 8
LORA_SCALE = 2.0
DEQUANT = float(np.float32(1.0 / 127.0))
QK_SCALE = float(1.0 / np.sqrt(HD))
LN_EPS, RMS_EPS = 1e-5, 1e-6

PAIRS = HEADS // 2
PARTS = 3
TERMS = 6
Q_PART = (0, 0, 0, 1, 1, 2)
K_PART = (0, 1, 2, 0, 1, 0)
KROWS = HD * TERMS
MROWS = 2
QROWS = 2 * KROWS

STEPS = 32
LEAD = 19
UNITS = 2 * STEPS
RING = 16
BANKS = 3

X_PE = ((1, "xt0"), (3, "q0"), (4, "m01"), (5, "k0"), (7, "qt"), (8, "kt"), (11, "pr1"), (12, "m02"), (14, "v1"),
        (19, "xt3"), (20, "m03"), (21, "rt"), (27, "ct"), (28, "m10"), (29, "out"))
Y_PE = ((4, "m11"), (7, "v0"), (9, "pr0"), (12, "m12"), (13, "xt1"), (14, "g0"), (15, "u0"), (16, "g1"),
        (17, "u1"), (18, "g2"), (19, "u2"), (20, "m13"), (21, "dn"), (25, "xt2"), (26, "qka"), (27, "qkb"),
        (28, "m00"))
PIECE = {"qt": (-1, "M2"), "kt": (-1, "M2"), "v1": (-1, "M2"),
         "xt0": (1, "P0"), "q0": (1, "P0"), "k0": (1, "P0"), "v0": (1, "V0"),
         "pr1": (-2, "E"), "xt3": (-2, "E"), "rt": (-2, "E"), "ct": (-2, "E"), "out": (-2, "E"),
         "m01": (0, "MXt"), "m02": (0, "MXt"), "m03": (0, "MXt"), "m10": (-1, "MXh"),
         "m11": (-1, "MXt"), "m12": (-1, "MXt"), "m13": (-1, "MXt"), "m00": (1, "MXh"),
         "pr0": (0, "M1"), "xt1": (0, "M1"), "g0": (0, "M1"), "u0": (0, "M1"), "g1": (0, "M1"), "u1": (0, "M1"),
         "g2": (0, "M1"), "u2": (0, "M1"), "dn": (0, "M1"), "xt2": (0, "M1"), "qka": (0, "M1"), "qkb": (0, "M1")}


def sem_name(piece):
    return piece[0:2] if piece[0] == "m" else piece


def count(piece, b):
    return 4 * b + int(piece[2]) + 1 if piece[0] == "m" else b + 1


def parts_of(kind, i):
    if kind == "X":
        have = (("A", i < BATCH), ("At", i >= 2), ("MXt", i < BATCH),
                ("MXh", 1 <= i <= BATCH), ("M2", 1 <= i <= BATCH), ("P0", i + 1 < BATCH), ("E", i >= 2))
    else:
        have = (("A", 1 <= i <= BATCH), ("At", 0 <= i < BATCH), ("MXt", 1 <= i <= BATCH),
                ("MXh", i + 1 < BATCH), ("M1", 0 <= i < BATCH), ("V0", i + 1 < BATCH), ("S0", i + 2 < BATCH))
    return frozenset(n for n, yes in have if yes)


def slot_pieces(kind, i):
    have = parts_of(kind, i)
    return [(s, n) for s, n in (X_PE if kind == "X" else Y_PE) if PIECE[n][1] in have]


SLOTS = [("Y", -1)] + [(k, i) for i in range(BATCH + 2) for k in "XY" if (k, i) != ("Y", BATCH + 1)]
LOOP_FROM, LOOP_TO = 2, BATCH - 2
assert all(parts_of("X", i) == parts_of("X", 2) and parts_of("Y", i) == parts_of("Y", 2)
           for i in range(LOOP_FROM, LOOP_TO))


def piece_before(kind, i, name):
    seen = []
    for k, j in SLOTS:
        for _, n in slot_pieces(k, j):
            if (k, j, n) == (kind, i, name):
                return (seen[-1][0], seen[-1][1] - i) if seen else None
            seen.append((n, j + PIECE[n][0]))
    raise AssertionError(name)


def attends_before(layer, b):
    if isinstance(b, int):
        return (max(2 * b - 1, 0) if layer == 0 else min(2 * b + 2, 2 * BATCH - 1))
    return 2 * b - 1 if layer == 0 else 2 * b + 2


def maxima_before(layer, b):
    return attends_before(layer, b)


def bank_of(layer, n):
    return (n + layer) % BANKS


def free_at(layer, n, b, base):
    if isinstance(b, int) and n == 0 and (layer, b) in ((0, 1), (1, BATCH - 1)):
        return base
    if layer == 0 and n < 2:
        return base + n - 1
    return base + n - 2


def wide(ap, dim, n):
    shape = list(ap.shape)
    shape[dim] = n
    return ap.broadcast_to(shape)


def need(eng, sem, value):
    if isinstance(value, int) and value <= 0:
        return
    eng.wait_ge(sem, value)


def wait_apart(eng, sem, value, passed):
    need(eng, sem, value)
    if not isinstance(value, int):
        eng.sem_inc(passed, 1)


def build(nc, T, out_dram):
    ctx = ExitStack()
    with ctx:
        def sb(name, shape, dt=F32):
            return ctx.enter_context(nc.sbuf_tensor(name, shape, dt))

        def sem(name):
            return ctx.enter_context(nc.semaphore(name))

        q_rows = [nc.dram_tensor(f"q_rows{l}", (128, TERMS, SEQ), BF16).ap() for l in (0, 1)]
        k_rows = [nc.dram_tensor(f"k_rows{l}", (128, TERMS, SEQ), BF16).ap() for l in (0, 1)]
        rden_rows = [nc.dram_tensor(f"rden_rows{l}", (2, 8, SEQ), F32).ap() for l in (0, 1)]

        ident = sb("ident", [128, 128])
        wq = sb("wq", [128, D])
        wk = sb("wk", [128, D])
        wv = sb("wv", [128, D])
        qk_bias = sb("qk_bias", [128, 2])
        bq_scaled = sb("bq_scaled", [128, 1])
        v_bias = [sb(f"v_bias{l}", [128, TT * D]) for l in (0, 1)]
        wo = [sb(f"wo{l}", [128, 2, D]) for l in (0, 1)]
        w_gate = sb("w_gate", [128, NH, 128])
        w_up = sb("w_up", [128, NH, 128])
        w_down = sb("w_down", [128, NH, D])
        wqkv = sb("wqkv", [128, 3 * D])
        qk1_bias = sb("qk1_bias", [128, 2 * D])
        norm_w = sb("norm_w", [128, 2])
        qn_scaled = sb("qn_scaled", [128, 1])
        w_base = sb("w_base", [128, D])
        w_mid = sb("w_mid", [128, 2 * EXPERTS])
        mid_bias = sb("mid_bias", [128, 2 * EXPERTS])
        w_lora = sb("w_lora", [EXPERTS * RANK + 1, D])
        half_neg = sb("half_neg", [128, TT])

        x_in = sb("x_in", [128, TT, D])
        res = [sb(f"res{l}", [128, TT, D]) for l in (0, 1)]
        x1 = sb("x1", [128, TT, D])
        x2 = sb("x2", [128, TT, D])
        x3 = sb("x3", [128, TT, D])
        bn = [sb(f"bn{k}", [128, TT, 6]) for k in range(4)]
        mv = [sb(f"mv{k}", [128, TT, 2]) for k in range(4)]
        vpe = [sb(f"vpe{k}", [128, TT]) for k in range(4)]
        rstd = [sb(f"rstd{k}", [128, TT]) for k in range(4)]
        neg_mean = [sb(f"neg_mean{k}", [128, TT]) for k in range(4)]
        shift = [sb(f"shift{k}", [128, TT]) for k in range(4)]
        xn = [sb(f"xn{k}", [128, TT, D]) for k in (0, 1, 3)]
        xn.insert(2, xn[1])
        xnt = [sb(f"xnt{k}", [128, SEQ]) for k in range(4)]

        qf = [[sb(f"{c}f{l}", [128, SEQ]) for c in "qk"] for l in (0, 1)]
        qp = [[sb(f"{c}p{l}", [128, PARTS, SEQ], BF16) for c in "qk"] for l in (0, 1)]
        q_stack = [sb(f"q_stack{l}", [128, PAIRS, SEQ], BF16) for l in (0, 1)]
        k_stack = [[sb(f"k_stack{l}{e}", [128, PAIRS, SEQ], BF16) for e in (0, 1)] for l in (0, 1)]
        v_aug = [sb(f"v_aug{l}", [128, TT, HEADS, 32]) for l in (0, 1)]
        neg_max = [sb(f"neg_max{l}", [128, 4, 32]) for l in (0, 1)]
        neg_high = [sb(f"neg_high{l}", [128, 4, 16], BF16) for l in (0, 1)]
        m_parts = [[sb(f"m_parts{l}{k}", [32, 128], BF16) for k in (0, 1)] for l in (0, 1)]
        probs = sb("probs", [128, RING, SEQ])
        o_raw = [sb(f"o_raw{l}", [128, 2, SEQ]) for l in (0, 1)]
        rden_all = [sb(f"rden_all{l}", [128, 2, SEQ]) for l in (0, 1)]
        den = [sb(f"den{l}", [128, 2, 32]) for l in (0, 1)]
        rden = [sb(f"rden{l}", [128, 2, 32]) for l in (0, 1)]

        th = sb("th", [128, SEQ])
        gs = sb("gs", [128, SEQ])
        up = sb("up", [128, SEQ])
        ht = sb("ht", [128, NH, SEQ])
        qk1 = sb("qk1", [128, TT, 2 * D])
        sq = ht[:, 0:2, :].rearrange("p c (t n) -> p (c t) n", n=2 * D)
        ms = sb("ms", [128, TT * 32])
        nw_y = sb("nw_y", [128, TT * 32])
        nw_t = sb("nw_t", [128, TT * 32])
        nw_u = sb("nw_u", [128, TT * 32])

        rm = sb("rm", [128, TT, 2 * EXPERTS])
        lmax = sb("lmax", [128, TT])
        lsh = sb("lsh", [128, TT, EXPERTS])
        lexp = sb("lexp", [128, TT, EXPERTS])
        lsum = sb("lsum", [128, TT])
        lrec = sb("lrec", [128, TT])
        gating = sb("gating", [128, TT, EXPERTS], BF16)
        coef = sb("coef", [128, TT, EXPERTS * RANK])
        coef_t = sb("coef_t", [EXPERTS * RANK + 1, SEQ])

        stage = probs[:, :, :].rearrange("p a b -> p (a b)")
        wo_nat = [stage[:, l * 128:(l + 1) * 128] for l in (0, 1)]
        wo_perm = [stage[:, 256 + l * 256:512 + l * 256] for l in (0, 1)]
        bo_col = [stage[:, 768 + l:769 + l] for l in (0, 1)]
        int_w = [stage[:, 1024 + 384 * n:1408 + 384 * n].bitcast(I32) for n in range(3)]
        flt_w = [stage[:, 2304 + 384 * n:2688 + 384 * n] for n in range(3)]
        wqkv_nat = stage[:, 3584:3968]
        base_nat = stage[:, 3968:4096]
        router_nat = stage[0:EXPERTS, 4096:4224]
        lora_nat = stage[0:EXPERTS * RANK, 4224:4352]

        ps = ctx.enter_context(nc.psum_tensor("ps", [128, 8, 512], F32))
        acc = ps[:, 6, :]
        gen = ps[:, 7, :]
        gen4 = gen.rearrange("p (t n) -> p t n", t=TT)

        first_loaded = sem("first_loaded")
        w_loaded = sem("w_loaded")
        k_zeros = sem("k_zeros")
        z_done = sem("z_done")
        k_both = sem("k_both")
        k_ones = sem("k_ones")
        v_zeros = [sem(f"v_zeros{l}") for l in (0, 1)]
        wo_zeros = sem("wo_zeros")
        bq_ready = sem("bq_ready")
        ident_zero = sem("ident_zero")
        ident_ready = sem("ident_ready")
        w_placed = sem("w_placed")
        w_turned = sem("w_turned")
        w_ready = sem("w_ready")
        names = sorted({sem_name(n) for n in PIECE})
        written = {n: sem(f"{n}_written") for n in names}
        read = {n: sem(f"{n}_read") for n in names}
        x_loaded = sem("x_loaded")
        res_copied = [sem(f"res_copied{l}") for l in (0, 1)]
        bn_done = [sem(f"bn_done{k}") for k in range(4)]
        mv_done = [sem(f"mv_done{k}") for k in range(4)]
        var_ready = [sem(f"var_ready{k}") for k in range(4)]
        rstd_ready = [sem(f"rstd_ready{k}") for k in range(4)]
        shift_ready = [sem(f"shift_ready{k}") for k in range(4)]
        xn_ready = [sem(f"xn_ready{k}") for k in range(4)]
        resid1 = [sem(f"{c}_resid1") for c in ("q0", "k0", "q1", "k1")]
        part0 = [sem(f"part0_{l}") for l in (0, 1)]
        part1 = [sem(f"{c}_part1") for c in ("q0", "k0", "q1", "k1")]
        part2 = [sem(f"{c}_part2") for c in ("q0", "k0", "q1", "k1")]
        rows_out = [[sem(f"{c}rows_out{l}") for c in "qk"] for l in (0, 1)]
        stack_in = [[sem(f"stack_in{l}{h}") for h in (0, 1)] for l in (0, 1)]
        high_done = sem("high_done")
        low_done = [sem(f"low_done{l}") for l in (0, 1)]
        m_in = [[sem(f"m_in{l}{q}") for q in range(4)] for l in (0, 1)]
        max_scores = sem("max_scores")
        max_taken = sem("max_taken")
        scores = sem("scores")
        exps = sem("exps")
        pv = sem("pv")
        o_saved = sem("o_saved")
        den_in = [sem(f"den_in{l}") for l in (0, 1)]
        rden_ready = [sem(f"rden_ready{l}") for l in (0, 1)]
        rden_out = [sem(f"rden_out{l}") for l in (0, 1)]
        rden_in = [sem(f"rden_in{l}") for l in (0, 1)]
        att_ready = [sem(f"att_ready{l}") for l in (0, 1)]
        tanh_done = sem("tanh_done")
        ht_done = sem("ht_done")
        squared = sem("squared")
        newton = sem("newton")
        qk_normed = [sem(f"{c}_normed") for c in "qk"]
        moe = sem("moe")
        l_exp = sem("l_exp")
        m_rec = sem("m_rec")
        gate_ready = sem("gate_ready")
        coef_ready = sem("coef_ready")
        stored = sem("stored")
        passed = sem("passed")
        N_NEWTON = 14

        block = ctx.enter_context(nc.Block())

        def walk(eng, slot):
            for k, i in SLOTS:
                if LOOP_FROM <= i < LOOP_TO:
                    if (k, i) == ("X", LOOP_FROM):
                        with eng.Fori(LOOP_FROM, LOOP_TO) as it:
                            slot("X", it, LOOP_FROM)
                            slot("Y", it, LOOP_FROM)
                else:
                    slot(k, i, i)

        @block.sync
        def _(sp):
            def hold(sem, value):
                wait_apart(sp, sem, value, passed)

            def first_load(dst, src):
                sp.dma_start(dst, src).then_inc(first_loaded, 16)

            def load(dst, src):
                sp.dma_start(dst, src).then_inc(w_loaded, 16)

            sp.dma_start(x_in[:, :, :], T["L0_attn_x"][0].rearrange("(t p) d -> p t d", p=128)).then_inc(x_loaded, 16)
            first_load(wq[:, :].rearrange("d (h e) -> d h e", h=HEADS), T["L0_attn_wq"].rearrange("h d e -> d h e"))
            first_load(wk[:, :].rearrange("d (h e) -> d h e", h=HEADS), T["L0_attn_wk"].rearrange("h d e -> d h e"))
            first_load(wv[:, :].rearrange("d (h e) -> d h e", h=HEADS), T["L0_attn_wv"].rearrange("h d e -> d h e"))
            first_load(qk_bias[:, 0:1], bass.AP(T["L0_attn_bq"].tensor, 0, [[1, 128], [1, 1]]))
            first_load(qk_bias[:, 1:2], bass.AP(T["L0_attn_bk"].tensor, 0, [[1, 128], [1, 1]]))
            first_load(v_bias[0][:, :], bass.AP(T["L0_attn_bv"].tensor, 0, [[0, 128], [0, TT], [1, 128]]))
            load(wo_nat[0], T["L0_attn_wo"])
            load(wo_nat[1], T["L1_attn_Wproj"])
            load(bo_col[0], bass.AP(T["L0_attn_bo"].tensor, 0, [[1, 128], [1, 1]]))
            load(bo_col[1], bass.AP(T["L1_attn_bproj"].tensor, 0, [[1, 128], [1, 1]]))
            load(int_w[0].rearrange("p (c f) -> p c f", c=NH), T["L0_ffn_w_gate"].rearrange("(c p) f -> p c f", p=128))
            load(int_w[1].rearrange("p (c f) -> p c f", c=NH), T["L0_ffn_w_up"].rearrange("(c p) f -> p c f", p=128))
            load(int_w[2], T["L0_ffn_w_down"])
            load(wqkv_nat.rearrange("p (c f) -> p c f", c=3), T["L1_attn_Wqkv"].rearrange("(c p) f -> p c f", p=128))
            load(qk1_bias[:, :], bass.AP(T["L1_attn_bqkv"].tensor, 0, [[0, 128], [1, 256]]))
            load(v_bias[1][:, :], bass.AP(T["L1_attn_bqkv"].tensor, 256, [[0, 128], [0, TT], [1, 128]]))
            load(norm_w[:, 0:1], bass.AP(T["L1_attn_qn_w"].tensor, 0, [[0, HEADS], [1, HD], [1, 1]]))
            load(norm_w[:, 1:2], bass.AP(T["L1_attn_kn_w"].tensor, 0, [[0, HEADS], [1, HD], [1, 1]]))
            load(base_nat, T["L1_ffn_base_w"])
            load(router_nat, T["L1_ffn_router_w"])
            load(w_mid[:, EXPERTS:], T["L1_ffn_lora_A"])
            load(lora_nat, T["L1_ffn_lora_B"].rearrange("e r d -> (e r) d"))
            load(w_lora[64:65, :], bass.AP(T["L1_ffn_base_b"].tensor, 0, [[0, 1], [1, 128]]))
            load(mid_bias[:, 0:EXPERTS], bass.AP(T["L1_ffn_router_b"].tensor, 0, [[0, 128], [1, 8]]))
            def tokens(b):
                x = T["L0_attn_x"]
                return (x[b:b + 1] if isinstance(b, int) else x[bass.ds(b, 1)]).rearrange("a (t p) d -> p (a t) d", p=128)

            def load_x(b):
                if not isinstance(b, int) or b > 0:
                    hold(xn_ready[0], b)
                sp.dma_start(x_in[:, :, :], tokens(b)).then_inc(x_loaded, 16)

            def load_res0(b):
                if not isinstance(b, int) or b > 0:
                    hold(read["pr0"], b)
                sp.dma_start(res[0][:, :, :], tokens(b)).then_inc(res_copied[0], 16)

            load_res0(0)
            load_x(1)

            def parts_out(l, which, b):
                for n in which:
                    rows, pick = ((q_rows[l], Q_PART), (k_rows[l], K_PART))[n]
                    for h in (0, 1):
                        hold(stack_in[l][h], 64 * b)
                    hold(part2[2 * l + n], b + 1)
                    for j0, j1 in ((0, 3), (3, 5), (5, 6)):
                        step = pick[j0 + 1] - pick[j0] if j1 - j0 > 1 else 0
                        sp.dma_start(rows[:, j0:j1, :],
                                     bass.AP(qp[l][n][:, :, :].tensor, pick[j0] * SEQ,
                                             [[PARTS * SEQ, 128], [step * SEQ, j1 - j0], [1, SEQ]])
                                     ).then_inc(rows_out[l][n], 16)

            def stack_half(l, half, b):
                for n in (0, 1):
                    hold(rows_out[l][n], 48 * (b + 1))
                if not isinstance(b, int) or b > 0:
                    hold(scores, UNITS * attends_before(l, b - 1) + 32 * (half + 1))
                for rows, stacks in ((q_rows[l], (q_stack[l], q_stack[l])), (k_rows[l], k_stack[l])):
                    for e in (0, 1):
                        src = bass.AP(rows.tensor, (64 * e + 32 * half) * TERMS * SEQ,
                                      [[SEQ, KROWS], [HD * TERMS * SEQ, 4], [1, SEQ]])
                        sp.dma_start(stacks[e][KROWS * e:KROWS * e + KROWS, 4 * half:4 * half + 4, :], src
                                     ).then_inc(stack_in[l][half], 16)

            def max_rows(l, quarter, b):
                hold(read[f"m{l}"], 4 * b + quarter + 1)
                sp.dma_start(q_stack[l][QROWS:QROWS + 2 * MROWS, 2 * quarter:2 * quarter + 2, :],
                             m_parts[l][quarter % 2][:, :]).then_inc(m_in[l][quarter], 16)

            def den_lines(l, c, b):
                hold(o_saved, 2 * attends_before(l, b) + c + 1)
                sp.dma_start(den[l][:, c, :],
                             bass.AP(o_raw[l][:, :, :].tensor, 8 * 2 * SEQ + c * SEQ, [[16 * 2 * SEQ, 8], [32, 16], [1, 32]])
                             ).then_inc(den_in[l], 16)

            def rden_lines(l, c, b):
                hold(rden_ready[l], 2 * b + c + 1)
                hold(rden_in[l], 16 * (2 * b + c))
                sp.dma_start(bass.AP(rden_rows[l].tensor, c * 8 * SEQ, [[32, 128], [1, 32]]), rden[l][:, c, :]
                             ).then_inc(rden_out[l], 16)
                hold(rden_out[l], 16 * (2 * b + c + 1))
                hold(att_ready[l], 2 * b + c)
                sp.dma_start(rden_all[l][:, c, :],
                             bass.AP(rden_rows[l].tensor, c * 8 * SEQ, [[SEQ, 8], [0, 16], [1, SEQ]])
                             ).then_inc(rden_in[l], 16)

            def slot(kind, i, at):
                have = parts_of(kind, at)
                if kind == "X":
                    if 0 <= at and at + 2 < BATCH:
                        load_x(i + 2)
                    if "E" in have:
                        den_lines(1, 1, i - 2)
                    if "MXt" in have:
                        max_rows(0, 1, i)
                    if "E" in have:
                        rden_lines(1, 1, i - 2)
                    if "M2" in have:
                        parts_out(1, (0, 1), i - 1)
                    if "MXt" in have:
                        max_rows(0, 2, i)
                    if at == 1:
                        hold(k_ones, 4)
                    if "M2" in have:
                        stack_half(1, 0, i - 1)
                        stack_half(1, 1, i - 1)
                    if "P0" in have:
                        parts_out(0, (0, 1), i + 1)
                    if "A" in have:
                        den_lines(0, 0, i)
                    if "MXt" in have:
                        max_rows(0, 3, i)
                    if "M2" in have:
                        hold(read["dn"], i)
                        if "E" in have:
                            hold(read["pr1"], i - 1)
                        sp.dma_start(res[1][:, :, :], x2[:, :, :]).then_inc(res_copied[1], 16)
                    if "P0" in have:
                        stack_half(0, 0, i + 1)
                    if "MXh" in have:
                        max_rows(1, 0, i - 1)
                    if "A" in have:
                        rden_lines(0, 0, i)
                    if "E" in have:
                        hold(read["out"], i - 1)
                        dst = out_dram[at - 2:at - 1] if isinstance(i, int) else out_dram[bass.ds(i - 2, 1)]
                        sp.dma_start(dst.rearrange("a (t p) d -> p (a t) d", p=128), x3[:, :, :]).then_inc(stored, 16)
                    if "P0" in have:
                        stack_half(0, 1, i + 1)
                else:
                    if at == -1:
                        parts_out(0, (0, 1), 0)
                        hold(k_ones, 2)
                        stack_half(0, 0, 0)
                        stack_half(0, 1, 0)
                        max_rows(0, 0, 0)
                        return
                    if "M1" in have:
                        den_lines(0, 1, i)
                    if "MXt" in have:
                        max_rows(1, 1, i - 1)
                    if "M1" in have:
                        rden_lines(0, 1, i)
                    if "MXt" in have:
                        max_rows(1, 2, i - 1)
                    if "V0" in have:
                        load_res0(i + 1)
                    if "A" in have:
                        den_lines(1, 0, i - 1)
                    if "MXt" in have:
                        max_rows(1, 3, i - 1)
                    if "A" in have:
                        rden_lines(1, 0, i - 1)
                    if "MXh" in have:
                        max_rows(0, 0, i + 1)

            walk(sp, slot)
            hold(stored, 16 * BATCH)

        @block.gpsimd
        def _(pool):
            pool.memset(half_neg[:, :], -0.5).then_inc(ident_zero, 1)
            pool.memset(ident[:, :], 0.0).then_inc(ident_zero, 1)
            pool.wait_ge(ident_zero, 2)
            pool.affine_select(out=ident[:, :], in_=ident[:, :], compare_op=ALU.not_equal, fill=1.0, base=0,
                               pattern=[[-1, 128]], channel_multiplier=1).then_inc(ident_ready, 1)
            pool.memset(mid_bias[:, EXPERTS:], 0.0)
            def norm_factors(k, b):
                pool.wait_ge(var_ready[k], b + 1)
                pool.tensor_tensor(rstd[k][:, :], vpe[k][:, :], half_neg[:, :], ALU.pow).then_inc(rstd_ready[k], 1)
                pool.wait_ge(rstd_ready[k], b + 1)
                pool.tensor_tensor(shift[k][:, :], neg_mean[k][:, :], rstd[k][:, :], ALU.mult).then_inc(shift_ready[k], 1)

            def residual1(l, n, b):
                pool.wait_ge(part0[l], 2 * b + n + 1)
                pool.tensor_tensor(qf[l][n][:, :], qf[l][n][:, :], qp[l][n][:, 0, :], ALU.subtract
                                   ).then_inc(resid1[2 * l + n], 1)

            def residual2(l, n, b):
                pool.wait_ge(part1[2 * l + n], b + 1)
                pool.tensor_tensor(qp[l][n][:, 2, :], qf[l][n][:, :], qp[l][n][:, 1, :], ALU.subtract
                                   ).then_inc(part2[2 * l + n], 1)

            def normalise(l, c, b):
                pool.wait_ge(rden_in[l], 16 * (2 * b + c + 1))
                pool.tensor_tensor(o_raw[l][:, c, :], o_raw[l][:, c, :], rden_all[l][:, c, :], ALU.mult
                                   ).then_inc(att_ready[l], 1)

            def scale_qk(n, b):
                if n == 0:
                    pool.wait_ge(newton, N_NEWTON * (b + 1))
                x = qk1[:, :, D * n:D * n + D].rearrange("p t (h e) -> p t h e", e=HD)
                inv = nw_y[:, :].rearrange("p (t n h) -> p t n h", t=TT, n=2)[:, :, n, :]
                for t in range(TT):
                    last = pool.tensor_tensor(x[:, t, :, :], x[:, t, :, :], wide(inv[:, t, :, None], 2, HD), ALU.mult)
                last.then_inc(qk_normed[n], 1)

            def up_mul(c, b):
                pool.wait_ge(read[f"g{c}"], b + 1)
                pool.wait_ge(read[f"u{c}"], b + 1)
                pool.tensor_tensor(ht[:, c, :], up[:, :], gs[:, :], ALU.mult).then_inc(ht_done, 1)

            def mix(b):
                pool.wait_ge(gate_ready, b + 1)
                need(pool, read["ct"], b)
                for t in range(TT):
                    last = pool.tensor_tensor(coef[:, t, :].rearrange("p (e r) -> p e r", r=RANK),
                                              wide(gating[:, t, :, None], 2, RANK),
                                              wide(rm[:, t, None, EXPERTS:], 1, EXPERTS), ALU.mult)
                last.then_inc(coef_ready, 1)

            def slot(kind, i, at):
                have = parts_of(kind, at)
                if kind == "X":
                    if "M2" in have:
                        scale_qk(0, i - 1)
                        scale_qk(1, i - 1)
                    if "E" in have:
                        normalise(1, 1, i - 2)
                    if "M2" in have:
                        for n in (0, 1):
                            residual1(1, n, i - 1)
                            residual2(1, n, i - 1)
                    if "P0" in have:
                        for n in (0, 1):
                            residual1(0, n, i + 1)
                        for n in (0, 1):
                            residual2(0, n, i + 1)
                    if "E" in have:
                        norm_factors(3, i - 2)
                        mix(i - 2)
                    if "A" in have:
                        normalise(0, 0, i)
                else:
                    if at == -1:
                        norm_factors(0, 0)
                        for n in (0, 1):
                            residual1(0, n, 0)
                            residual2(0, n, 0)
                    if at == -1:
                        norm_factors(0, 1)
                    if at == -1:
                        for t in (*k_stack[1], q_stack[1]):
                            pool.memset(t[:, :, :].rearrange("p a b -> p (a b)").bitcast(F32), 0.0).then_inc(k_zeros, 1)
                    if "M1" in have:
                        normalise(0, 1, i)
                        norm_factors(1, i)
                        for c in range(NH):
                            up_mul(c, i)
                    if "S0" in have and at >= 0:
                        norm_factors(0, i + 2)
                    if "M1" in have:
                        norm_factors(2, i)
                    if "A" in have:
                        normalise(1, 0, i - 1)

            walk(pool, slot)

        @block.scalar
        def _(act):
            def copy(dst, src):
                return act.activation(dst, src, ACT.Copy)

            def weights_out():
                act.wait_ge(w_turned, 1)
                for l in (0, 1):
                    copy(wo[l][:, :, :], ps[:, 0, 256 * l:256 * l + 256].rearrange("p (c n) -> p c n", c=2))
                copy(w_gate[:, :, :], ps[:, 1, 0:384].rearrange("p (c n) -> p c n", c=3))
                copy(w_up[:, :, :], ps[:, 2, 0:384].rearrange("p (c n) -> p c n", c=3))
                copy(w_down[:, :, :], ps[:, 3, 0:384].rearrange("p (c n) -> p c n", c=3))
                copy(wqkv[:, :], ps[:, 4, 0:384])
                copy(w_base[:, :], ps[:, 5, 0:128])
                copy(w_mid[:, 0:EXPERTS], ps[:, 5, 128:136]).then_inc(w_ready, 1)

            def exp_unit(l, u, b):
                a = attends_before(l, b)
                act.wait_ge(scores, UNITS * a + u + 1)
                if u % 4 == 0 and not (isinstance(a, int) and a == 0 and u < RING):
                    act.wait_ge(pv, 16 * a + (u - RING) // 4 + 1)
                act.activation(probs[:, u % RING, :], ps[:, bank_of(l, u), :], ACT.Exp).then_inc(exps, 1)

            def apply_norm(k, x, tiles, b):
                act.wait_ge(shift_ready[k], b + 1)
                for t in tiles:
                    last = act.activation(xn[k][:, t, :], x[:, t, :], ACT.Identity, bias=shift[k][:, t:t + 1],
                                          scale=rstd[k][:, t:t + 1])
                if tiles[-1] == TT - 1:
                    last.then_inc(xn_ready[k], 1)

            def save_out(l, half, b):
                act.wait_ge(pv, 16 * attends_before(l, b) + 8 * (half + 1))
                need(act, read[("pr0", "pr1")[l]], b)
                copy(o_raw[l][:, half, :], acc).then_inc(o_saved, 1)

            def take(name, dst, b):
                act.wait_ge(written[name], b + 1)
                copy(dst, gen).then_inc(read[name], 1)

            def take_qk(l, n, b):
                name = (("q0", "k0"), ("qt", "kt"))[l][n]
                act.wait_ge(written[name], b + 1)
                if l == 0:
                    bias = (bq_scaled[:, 0:1], qk_bias[:, 1:2])[n]
                    kw = dict(scale=(QK_SCALE, 1.0)[n], bias=bias)
                else:
                    kw = dict(scale=(qn_scaled[:, 0:1], norm_w[:, 1:2])[n])
                act.activation(qf[l][n][:, :], gen, ACT.Identity, **kw).then_inc(read[name], 1)

            def take_part0(l, n, b):
                act.wait_ge(read[(("q0", "k0"), ("qt", "kt"))[l][n]], b + 1)
                need(act, rows_out[l][n], 48 * b)
                copy(qp[l][n][:, 0, :], qf[l][n][:, :]).then_inc(part0[l], 1)

            def take_part1(l, n, b):
                act.wait_ge(resid1[2 * l + n], b + 1)
                copy(qp[l][n][:, 1, :], qf[l][n][:, :]).then_inc(part1[2 * l + n], 1)

            def take_max(l, quarter, b):
                act.wait_ge(written[f"m{l}"], 4 * b + quarter + 1)
                if quarter < 2:
                    need(act, m_in[l][quarter + 2], 16 * b)
                else:
                    act.wait_ge(m_in[l][quarter - 2], 16 * (b + 1))
                copy(m_parts[l][quarter % 2][:, :], gen[0:32, 0:128]).then_inc(read[f"m{l}"], 1)

            def gate_tanh(c, b):
                act.wait_ge(written[f"g{c}"], b + 1)
                act.activation(th[:, :], gen, ACT.Tanh, scale=0.5).then_inc(tanh_done, 1)

            def take_up(c, b):
                act.wait_ge(written[f"u{c}"], b + 1)
                copy(up[:, :], gen).then_inc(read[f"u{c}"], 1)

            def square(half, b):
                act.wait_ge(read[("qka", "qkb")[half]], b + 1)
                act.activation(sq[:, 2 * half:2 * half + 2, :], qk1[:, 2 * half:2 * half + 2, :], ACT.Square
                               ).then_inc(squared, 1)

            def gate_exp(b):
                act.wait_ge(moe, 3 * (b + 1) + 1 * b)
                act.activation(lexp[:, :, :], lsh[:, :, :], ACT.Exp).then_inc(l_exp, 1)

            def take_coef(b):
                act.wait_ge(written["ct"], b + 1)
                need(act, read["out"], b)
                copy(coef_t[0:EXPERTS * RANK, :], gen[0:EXPERTS * RANK, :]).then_inc(read["ct"], 1)

            def slot(kind, i, at):
                have = parts_of(kind, at)
                if at == -1:
                    act.wait_ge(bq_ready, 1)
                    apply_norm(0, x_in, range(TT), 0)
                    take("xt0", xnt[0][:, :], 0)
                    for n in (0, 1):
                        take_qk(0, n, 0)
                        take_part0(0, n, 0)
                        take_part1(0, n, 0)
                    weights_out()
                    apply_norm(0, x_in, range(TT), 1)
                    take_max(0, 0, 0)
                    return
                for s in range(STEPS):
                    if "A" in have:
                        exp_unit(0 if kind == "X" else 1, 2 * s, i if kind == "X" else i - 1)
                    if s == 2 and "At" in have:
                        save_out(*((1, 1, i - 2) if kind == "X" else (0, 1, i)))
                    if s == 18 and "A" in have:
                        save_out(*((0, 0, i) if kind == "X" else (1, 0, i - 1)))
                    if "A" in have:
                        exp_unit(0 if kind == "X" else 1, 2 * s + 1, i if kind == "X" else i - 1)
                    for at_step, name in slot_pieces(kind, at):
                        if at_step == s and name[0] == "m":
                            take_max(int(name[1]), int(name[2]), i + PIECE[name][0])
                    if kind == "X":
                        if "P0" in have:
                            if s == 1:
                                take("xt0", xnt[0][:, :], i + 1)
                            if s in (3, 5):
                                take_qk(0, (s - 3) // 2, i + 1)
                            if s in (4, 6):
                                take_part0(0, (s - 4) // 2, i + 1)
                            if s in (14, 15):
                                take_part1(0, s - 14, i + 1)
                        if "M2" in have:
                            if s == 7:
                                take_qk(1, 0, i - 1)
                                take_part0(1, 0, i - 1)
                            if s == 8:
                                take_qk(1, 1, i - 1)
                            if s == 9:
                                take_part0(1, 1, i - 1)
                            if s in (10, 11):
                                take_part1(1, s - 10, i - 1)
                        if "E" in have:
                            if s in (17, 18):
                                apply_norm(3, x3, (2 * s - 34, 2 * s - 33), i - 2)
                            if s == 19:
                                take("xt3", xnt[3][:, :], i - 2)
                            if s == 23:
                                gate_exp(i - 2)
                            if s == 27:
                                take_coef(i - 2)
                    else:
                        if "S0" in have and s in (21, 22):
                            apply_norm(0, x_in, (2 * s - 42, 2 * s - 41), i + 2)
                        if "M1" in have:
                            if s == 12:
                                apply_norm(1, x1, range(TT), i)
                            if s == 13:
                                take("xt1", xnt[1][:, :], i)
                            if s in (14, 16, 18):
                                gate_tanh((s - 14) // 2, i)
                            if s in (15, 17, 19):
                                take_up((s - 15) // 2, i)
                            if s == 24:
                                apply_norm(2, x2, range(TT), i)
                            if s == 25:
                                take("xt2", xnt[2][:, :], i)
                            if s in (27, 28):
                                square(s - 27, i)

            walk(act, slot)

        @block.vector
        def _(dve):
            def zero_stacks(tiles):
                for t in tiles:
                    dve.memset(t[:, :, :].rearrange("p a b -> p (a b)").bitcast(F32), 0.0).then_inc(z_done, 1)
                dve.wait_ge(z_done, 3)

            def set_ones(l):
                k0, k1 = (t[:, :, :].rearrange("p a b -> p (a b)") for t in k_stack[l])
                dve.memset(k0[QROWS:QROWS + MROWS, :], 1.0).then_inc(k_ones, 1)
                dve.memset(k1[QROWS:QROWS + 2 * MROWS, :], 1.0).then_inc(k_both, 1)
                dve.wait_ge(k_both, l + 1)
                dve.memset(k1[QROWS:QROWS + MROWS, :], 0.0).then_inc(k_ones, 1)

            def clear_values(l):
                dve.memset(v_aug[l][:, :, :, :].rearrange("p a b c -> p (a b c)"), 0.0).then_inc(v_zeros[l], 1)
                dve.wait_ge(v_zeros[l], 1)
                for s in (0, 1):
                    dve.memset(v_aug[l][:, :, :, :].rearrange("p t (r s pp) m -> p (t r) s pp m", s=2, pp=2)
                               [:, :, s, :, 16 * s + HD:16 * s + HD + 1], 1.0)

            def place_weights():
                dve.memset(coef_t[64:65, :], 1.0)
                dve.wait_ge(w_loaded, 16 * 18)
                for l in (0, 1):
                    dve.memset(wo_perm[l], 0.0).then_inc(wo_zeros, 1)
                dve.wait_ge(wo_zeros, 2)
                for l in (0, 1):
                    for c in (0, 1):
                        for s in (0, 1):
                            dst = wo_perm[l][:, 128 * c:128 * c + 128].rearrange("n (pp e s d) -> n e pp s d", pp=2, e=2, s=2)
                            src = wo_nat[l].rearrange("n (e c s pp d) -> n e c s pp d", e=2, c=2, s=2, pp=2)
                            dve.tensor_copy(dst[:, :, :, s, 0:HD], src[:, :, c, s, :, :])
                    dve.tensor_copy(wo_perm[l][:, HD:HD + 1], bo_col[l])
                for n in range(3):
                    dve.tensor_scalar(flt_w[n], int_w[n], DEQUANT, (1.0, 1.0, 0.5)[n], ALU.mult, ALU.mult)
                dve.tensor_scalar(qn_scaled[:, :], norm_w[:, 0:1], QK_SCALE, None, ALU.mult)
                dve.tensor_scalar(w_lora[0:64, :], lora_nat, LORA_SCALE, None, ALU.mult).then_inc(w_placed, 1)

            def stats(k, x, b, tiles=range(TT)):
                if tiles[0] == 0:
                    need(dve, xn_ready[k], b)
                for t in tiles:
                    last = dve.bn_stats(bn[k][:, t, :], x[:, t, :])
                if tiles[-1] == TT - 1:
                    last.then_inc(bn_done[k], 1)

            def moments(k, b):
                wait_apart(dve, bn_done[k], b + 1, passed)
                for t in range(TT):
                    last = dve.bn_aggr(mv[k][:, t, :], bn[k][:, t, :])
                last.then_inc(mv_done[k], 1)

            def factors_in(k, b):
                dve.wait_ge(mv_done[k], b + 1)
                dve.tensor_scalar(neg_mean[k][:, :], mv[k][:, :, 0], -1.0, None, ALU.mult)
                dve.tensor_scalar(vpe[k][:, :], mv[k][:, :, 1], LN_EPS, None, ALU.add).then_inc(var_ready[k], 1)


            def max_tile(l, n, b):
                dve.wait_ge(max_scores, 2 * STEPS * maxima_before(l, b) + n + 1)
                pair, st, e = n // 8, (n // 2) % 4, n % 2
                col = 16 * e + 4 * (pair % 2) + st
                dve.tensor_reduce(neg_max[l][:, pair // 2, col:col + 1], ps[:, BANKS + bank_of(l, n), :], AX.X,
                                  ALU.max, negate=True).then_inc(max_taken, 1)

            def parts_high(l, quarter, b):
                dve.wait_ge(max_taken, 2 * STEPS * maxima_before(l, b) + 16 * (quarter + 1))
                dve.tensor_copy(neg_high[l][:, quarter, :].rearrange("p (e c) -> p e c", e=2),
                                neg_max[l][:, quarter, :].rearrange("p (e j c) -> p e j c", e=2, j=2)[:, :, 0, :]
                                ).then_inc(high_done, 1)

            def parts_low(l, quarter, b):
                dve.wait_ge(high_done, 4 * maxima_before(l, b) + quarter + 1)
                parts = neg_max[l][:, quarter, :].rearrange("p (e j c) -> p e j c", e=2, j=2)
                high = neg_high[l][:, quarter, :].rearrange("p (e c) -> p e c", e=2)
                dve.tensor_tensor(parts[:, :, 1, :], parts[:, :, 0, :], high, ALU.subtract).then_inc(low_done[l], 1)

            def take_v(l, s, b):
                name = ("v0", "v1")[l]
                dve.wait_ge(written[name], b + 1)
                src = gen.rearrange("p (r s m) -> p r s m", s=2, m=2 * HD)
                bias = v_bias[l][:, :].rearrange("p (r s m) -> p r s m", s=2, m=2 * HD)
                dst = v_aug[l][:, :, :, :].rearrange("p t (r s pp) m -> p (t r) s pp m", s=2, pp=2)
                last = dve.tensor_tensor(dst[:, :, s, :, 16 * s:16 * s + HD],
                                         src[:, :, s, :].rearrange("p r (pp d) -> p r pp d", d=HD),
                                         bias[:, :, s, :].rearrange("p r (pp d) -> p r pp d", d=HD), ALU.add)
                if s == 1:
                    last.then_inc(read[name], 1)

            def invert_den(l, c, b):
                dve.wait_ge(den_in[l], 16 * (2 * b + c + 1))
                need(dve, rden_out[l], 16 * (2 * b + c))
                dve.reciprocal(rden[l][:, c, :], den[l][:, c, :]).then_inc(rden_ready[l], 1)

            def add_into(name, dst, other, b):
                dve.wait_ge(written[name], b + 1)
                dve.tensor_tensor(dst[:, :, :], gen4, other[:, :, :], ALU.add).then_inc(read[name], 1)

            def project_add(l, dst, b):
                dve.wait_ge(res_copied[l], 16 * (b + 1))
                if l == 1:
                    need(dve, stored, 16 * b)
                add_into(("pr0", "pr1")[l], dst, res[l], b)

            def gate_mul(c, b):
                dve.wait_ge(tanh_done, NH * b + c + 1)
                need(dve, ht_done, NH * b + c)
                dve.scalar_tensor_tensor(out=gs[:, :], in0=th[:, :], scalar=1.0, in1=gen, op0=ALU.add,
                                         op1=ALU.mult).then_inc(read[f"g{c}"], 1)

            def down_add(b):
                need(dve, res_copied[1], 16 * b)
                add_into("dn", x2, x1, b)

            def take_qk1(half, b):
                name = ("qka", "qkb")[half]
                dve.wait_ge(written[name], b + 1)
                for t in (0, 1):
                    last = dve.tensor_tensor(qk1[:, 2 * half + t, :], gen[:, 256 * t:256 * t + 256], qk1_bias[:, :], ALU.add)
                last.then_inc(read[name], 1)

            def inverse_rms(first, count, b):
                for n in range(first, first + count):
                    if n < 2:
                        dve.wait_ge(squared, 2 * b + n + 1)
                        op = dve.tensor_reduce(ms[:, 64 * n:64 * n + 64],
                                               sq[:, 2 * n:2 * n + 2, :].rearrange("p t (g e) -> p (t g) e", e=HD),
                                               AX.X, ALU.add)
                    else:
                        dve.wait_ge(newton, N_NEWTON * b + n)
                        if n == 2:
                            op = dve.tensor_scalar(ms[:, :], ms[:, :], 1.0 / HD, RMS_EPS, ALU.mult, ALU.add)
                        elif n == 3:
                            op = dve.tensor_scalar(nw_t[:, :].bitcast(I32), ms[:, :].bitcast(I32), 1, None,
                                                   ALU.logical_shift_right)
                        elif n == 4:
                            op = dve.tensor_scalar(nw_y[:, :].bitcast(I32), nw_t[:, :].bitcast(I32), -1.0,
                                                   float(0x5f3759df), ALU.mult, ALU.add)
                        elif n % 3 == 2:
                            op = dve.tensor_tensor(nw_t[:, :], nw_y[:, :], nw_y[:, :], ALU.mult)
                        elif n % 3 == 0:
                            op = dve.scalar_tensor_tensor(out=nw_u[:, :], in0=nw_t[:, :], scalar=-0.5, in1=ms[:, :],
                                                          op0=ALU.mult, op1=ALU.mult)
                        else:
                            op = dve.scalar_tensor_tensor(out=nw_y[:, :], in0=nw_u[:, :], scalar=1.5, in1=nw_y[:, :],
                                                          op0=ALU.add, op1=ALU.mult)
                    op.then_inc(newton, 1)

            def route(link, b):
                if link == 0:
                    dve.wait_ge(written["rt"], b + 1)
                    dve.tensor_tensor(rm[:, :, :], gen[:, 0:TT * 16].rearrange("p (t n) -> p t n", t=TT),
                                      wide(mid_bias[:, None, :], 1, TT), ALU.add).then_inc(read["rt"], 1)
                elif link == 1:
                    dve.wait_ge(read["rt"], b + 1)
                    dve.tensor_reduce(lmax[:, :], rm[:, :, 0:EXPERTS], AX.X, ALU.max).then_inc(moe, 2)
                else:
                    dve.wait_ge(moe, 4 * b + 2)
                    dve.tensor_tensor(lsh[:, :, :], rm[:, :, 0:EXPERTS], wide(lmax[:, :, None], 2, EXPERTS),
                                      ALU.subtract).then_inc(moe, 1)

            def gates(link, b):
                if link == 0:
                    dve.wait_ge(l_exp, b + 1)
                    dve.tensor_reduce(lsum[:, :], lexp[:, :, :], AX.X, ALU.add).then_inc(moe, 1)
                elif link == 1:
                    dve.wait_ge(moe, 4 * b + 4)
                    dve.reciprocal(lrec[:, :], lsum[:, :]).then_inc(m_rec, 1)
                else:
                    dve.wait_ge(m_rec, b + 1)
                    dve.tensor_tensor(gating[:, :, :], lexp[:, :, :], wide(lrec[:, :, None], 2, EXPERTS), ALU.mult
                                      ).then_inc(gate_ready, 1)

            def finish(b):
                add_into("out", x3, x3, b)

            def slot(kind, i, at):
                have = parts_of(kind, at)
                tail, head = ((0, i), (1, i - 1)) if kind == "X" else ((1, i - 1), (0, i + 1))
                if at == -1:
                    dve.wait_ge(x_loaded, 16)
                    stats(0, x_in, 0)
                    moments(0, 0)
                    factors_in(0, 0)
                    dve.wait_ge(first_loaded, 16 * 6)
                    dve.tensor_scalar(bq_scaled[:, :], qk_bias[:, 0:1], QK_SCALE, None, ALU.mult).then_inc(bq_ready, 1)
                    zero_stacks((*k_stack[0], q_stack[0]))
                    place_weights()
                    set_ones(0)
                    clear_values(0)
                    for part in (0, 1):
                        take_v(0, part, 0)
                    dve.wait_ge(x_loaded, 32)
                    stats(0, x_in, 1)
                    moments(0, 1)
                    factors_in(0, 1)
                for h in range(2 * STEPS):
                    s, e = h // 2, h % 2
                    for work, step, l, b in (("MXt", s + STEPS - LEAD, *tail), ("MXh", s - LEAD, *head)):
                        if work in have and 0 <= step < STEPS:
                            max_tile(l, 2 * step + e, b)
                            if e == 1 and step % 8 == 7:
                                parts_high(l, step // 8, b)
                        if work in have and e == 0 and step % 8 == 0 and 0 < step <= STEPS:
                            parts_low(l, step // 8 - 1, b)
                    if kind == "X":
                        if "M2" in have:
                            if h < 11:
                                inverse_rms(3 + h, 1, i - 1)
                            if h in (29, 30):
                                take_v(1, h - 29, i - 1)
                        if "A" in have and h == 52:
                            invert_den(0, 0, i)
                        if "E" in have:
                            if h == 11:
                                invert_den(1, 1, i - 2)
                            if h == 23:
                                project_add(1, x3, i - 2)
                            if h in (25, 26):
                                if h == 25:
                                    dve.wait_ge(read["pr1"], i - 1)
                                stats(3, x3, i - 2, (0, 1) if h == 25 else (2, 3))
                            if h == 27:
                                moments(3, i - 2)
                            if h == 28:
                                factors_in(3, i - 2)
                            if h in (43, 44, 45):
                                route(h - 43, i - 2)
                            if h in (48, 49, 50):
                                gates(h - 48, i - 2)
                            if h == 59:
                                finish(i - 2)
                    elif at >= 0:
                        if "S0" in have:
                            if h == 30:
                                dve.wait_ge(x_loaded, 16 * (i + 3))
                            if h in (30, 32):
                                stats(0, x_in, i + 2, (0, 1) if h == 30 else (2, 3))
                            if h == 34:
                                moments(0, i + 2)
                            if h == 36:
                                factors_in(0, i + 2)
                        if "V0" in have and h in (16, 17):
                            take_v(0, h - 16, i + 1)
                        if "A" in have and h == 47:
                            invert_den(1, 0, i - 1)
                        if "M1" in have:
                            if h == 9:
                                invert_den(0, 1, i)
                            if h == 19:
                                project_add(0, x1, i)
                            if h == 20:
                                dve.wait_ge(read["pr0"], i + 1)
                                stats(1, x1, i)
                            if h == 21:
                                moments(1, i)
                                factors_in(1, i)
                            if at == 0 and h == 23:
                                clear_values(1)
                                dve.wait_ge(k_zeros, 3)
                                set_ones(1)
                            if h in (29, 33, 37):
                                gate_mul((h - 29) // 4, i)
                            if h == 43:
                                down_add(i)
                            if h == 44:
                                dve.wait_ge(read["dn"], i + 1)
                                stats(2, x2, i)
                            if h == 45:
                                moments(2, i)
                                factors_in(2, i)
                            if h in (53, 55):
                                take_qk1((h - 53) // 2, i)
                            if h in (57, 61):
                                inverse_rms((h - 57) // 4, 1, i)
                            if h >= 63:
                                inverse_rms(h - 61, 1, i)

            walk(dve, slot)

        @block.tensor
        def _(pe):
            def turn(dst, src, n=128):
                return pe.transpose(dst, src, ident[0:n, 0:n])

            def weights_turned():
                pe.wait_ge(w_placed, 1)
                for l in (0, 1):
                    for c in (0, 1):
                        turn(ps[:, 0, 256 * l + 128 * c:256 * l + 128 * c + 128], wo_perm[l][:, 128 * c:128 * c + 128])
                for n, w in enumerate((flt_w[0], flt_w[1], flt_w[2], wqkv_nat)):
                    for c in range(3):
                        turn(ps[:, 1 + n, 128 * c:128 * c + 128], w[:, 128 * c:128 * c + 128])
                turn(ps[:, 5, 0:128], base_nat)
                turn(ps[:, 5, 128:128 + EXPERTS], router_nat, EXPERTS).then_inc(w_turned, 1)
                pe.wait_ge(w_ready, 1)
                pe.wait_ge(k_ones, 2)

            pe.wait_ge(ident_ready, 1)

            def max_score(l, n, e, b):
                base = 2 * STEPS * maxima_before(l, b)
                if e == 0 and n % 16 == 0:
                    pe.wait_ge(stack_in[l][n // 16], 64 * (b + 1))
                need(pe, max_taken, free_at(l, 2 * n + e, b, base))
                tok, pair = 128 * (n % 4), n // 4
                pe.matmul(ps[:, BANKS + bank_of(l, 2 * n + e), :], q_stack[l][0:QROWS, pair, tok:tok + 128],
                          k_stack[l][e][0:QROWS, pair, :], start=True, stop=True).then_inc(max_scores, 1)

            def attend_score(l, u, b):
                group, kt, pp, e = u // 16, (u % 16) // 4, (u % 4) // 2, u % 2
                if u % 16 == 0:
                    pe.wait_ge(m_in[l][u // 16], 16 * (b + 1))
                need(pe, exps, free_at(l, u, b, UNITS * attends_before(l, b)))
                tok, pair = 128 * kt, 2 * group + pp
                pe.matmul(ps[:, bank_of(l, u), :], k_stack[l][e][:, pair, tok:tok + 128],
                          q_stack[l][:, pair, :], start=True, stop=True).then_inc(scores, 1)

            def attend_pv(l, u, b):
                group, kt = u // 16, (u % 16) // 4
                c, s = group // 2, group % 2
                a = attends_before(l, b)
                if u == 0:
                    pe.wait_ge(read[("v0", "v1")[l]], b + 1)
                if u % 32 == 0:
                    need(pe, o_saved, 2 * a + c)
                pe.wait_ge(exps, UNITS * a + u + 4)
                for j in range(4):
                    pp, e = j // 2, j % 2
                    last = pe.matmul(acc[32 * j:32 * j + 32, :], v_aug[l][:, kt, 8 * e + 2 * group + pp, :],
                                     probs[:, (u + j) % RING, :], start=(s == 0 and kt == 0),
                                     stop=(s == 1 and kt == TT - 1))
                last.then_inc(pv, 1)

            def turn_norm(k, b):
                pe.wait_ge(xn_ready[k], b + 1)
                for t in range(TT):
                    last = turn(gen[:, 128 * t:128 * t + 128], xn[k][:, t, :])
                return last

            def by_token(dst, xt, w, more=None):
                for t in range(TT):
                    last = pe.matmul(dst[:, t, :], xt[:, 128 * t:128 * t + 128], w, start=True, stop=more is None)
                    if more is not None:
                        last = pe.matmul(dst[:, t, :], more[0][:, 128 * t:128 * t + 128], more[1], start=False, stop=True)
                return last

            def project(l, b):
                pe.wait_ge(att_ready[l], 2 * b + 2)
                for t in range(TT):
                    for c in (0, 1):
                        last = pe.matmul(gen4[:, t, :], o_raw[l][:, c, 128 * t:128 * t + 128], wo[l][:, c, :],
                                         start=c == 0, stop=c == 1)
                return last

            def piece(name, i, at, kind, b):
                before = piece_before(kind, at, name)
                if before is not None:
                    pe.wait_ge(read[sem_name(before[0])], count(before[0], i + before[1]))
                if name in ("xt0", "xt1", "xt2", "xt3"):
                    last = turn_norm(int(name[2]), b)
                elif name in ("q0", "k0"):
                    pe.wait_ge(read["xt0"], b + 1)
                    last = pe.matmul(gen, (wq if name == "q0" else wk)[:, :], xnt[0][:, :], start=True, stop=True)
                elif name == "v0":
                    pe.wait_ge(read["xt0"], b + 1)
                    last = by_token(gen4, xnt[0], wv[:, :])
                elif name == "v1":
                    last = by_token(gen4, xnt[2], wqkv[:, 256:384])
                elif name[0] == "m":
                    l, quarter = int(name[1]), int(name[2])
                    pe.wait_ge(low_done[l], 4 * b + quarter + 1)
                    last = turn(gen[0:32, 0:128], neg_max[l][:, quarter, :])
                elif name in ("pr0", "pr1"):
                    last = project(int(name[2]), b)
                elif name[0] in "gu":
                    pe.wait_ge(read["xt1"], b + 1)
                    w = w_gate if name[0] == "g" else w_up
                    last = pe.matmul(gen, w[:, int(name[1]), :], xnt[1][:, :], start=True, stop=True)
                elif name == "dn":
                    pe.wait_ge(ht_done, NH * (b + 1))
                    for t in range(TT):
                        for c in range(NH):
                            last = pe.matmul(gen4[:, t, :], ht[:, c, 128 * t:128 * t + 128], w_down[:, c, :],
                                             start=c == 0, stop=c == NH - 1)
                elif name in ("qka", "qkb"):
                    pe.wait_ge(read["xt2"], b + 1)
                    half = int(name == "qkb")
                    for t in (0, 1):
                        tok = 128 * (2 * half + t)
                        last = pe.matmul(gen[:, 256 * t:256 * t + 256], xnt[2][:, tok:tok + 128], wqkv[:, 0:256],
                                         start=True, stop=True)
                elif name in ("qt", "kt"):
                    pe.wait_ge(qk_normed[int(name == "kt")], b + 1)
                    for t in range(TT):
                        c = 128 * (name == "kt")
                        last = turn(gen[:, 128 * t:128 * t + 128], qk1[:, t, c:c + 128])
                elif name == "rt":
                    pe.wait_ge(read["xt3"], b + 1)
                    last = by_token(gen[:, 0:TT * 16].rearrange("p (t n) -> p t n", t=TT), xnt[3], w_mid[:, :])
                elif name == "ct":
                    wait_apart(pe, coef_ready, b + 1, passed)
                    for t in range(TT):
                        last = turn(gen[0:64, 128 * t:128 * t + 128], coef[:, t, :])
                elif name == "out":
                    last = by_token(gen4, xnt[3], w_base[:, :], more=(coef_t, w_lora[:, :]))
                last.then_inc(written[sem_name(name)], 1)

            def slot(kind, i, at):
                have = parts_of(kind, at)
                pieces = slot_pieces(kind, at)
                if at == -1:
                    pe.wait_ge(first_loaded, 16 * 6)
                    for name in ("xt0", "q0", "k0", "v0"):
                        if name == "xt0":
                            last = turn_norm(0, 0)
                        elif name == "v0":
                            pe.wait_ge(read["k0"], 1)
                            last = by_token(gen4, xnt[0], wv[:, :])
                        else:
                            pe.wait_ge(read["xt0" if name == "q0" else "q0"], 1)
                            last = pe.matmul(gen, (wq if name == "q0" else wk)[:, :], xnt[0][:, :], start=True, stop=True)
                        last.then_inc(written[name], 1)
                    weights_turned()
                    pieces = [p for p in pieces if p[1] != "v0"]
                if (kind, at) == ("X", 1):
                    pe.wait_ge(k_ones, 4)
                tail, head = ((0, i), (1, i - 1)) if kind == "X" else ((1, i - 1), (0, i + 1))
                now, past = ((0, i), (1, i - 2)) if kind == "X" else ((1, i - 1), (0, i))
                for s in range(STEPS):
                    mx = None
                    if s < LEAD and "MXt" in have:
                        mx = (tail[0], s + STEPS - LEAD, tail[1])
                    if s >= LEAD and "MXh" in have:
                        mx = (head[0], s - LEAD, head[1])
                    for e in (0, 1):
                        if "A" in have:
                            attend_score(now[0], 2 * s + e, now[1])
                        if mx:
                            max_score(mx[0], mx[1], e, mx[2])
                    if s == 1 and "At" in have:
                        attend_pv(past[0], UNITS - 4, past[1])
                    if s % 2 and s > 1 and "A" in have:
                        attend_pv(now[0], 2 * s - 6, now[1])
                    for at_step, name in pieces:
                        if at_step == s:
                            piece(name, i, at, kind, i + PIECE[name][0])

            walk(pe, slot)


NAMES = ["L0_attn_x", "L0_attn_wq", "L0_attn_bq", "L0_attn_wk", "L0_attn_bk", "L0_attn_wv", "L0_attn_bv",
         "L0_attn_wo", "L0_attn_bo", "L0_ffn_w_gate", "L0_ffn_w_up", "L0_ffn_w_down", "L1_attn_Wqkv",
         "L1_attn_bqkv", "L1_attn_Wproj", "L1_attn_bproj", "L1_attn_qn_w", "L1_attn_kn_w", "L1_ffn_base_w",
         "L1_ffn_base_b", "L1_ffn_lora_A", "L1_ffn_lora_B", "L1_ffn_router_w", "L1_ffn_router_b"]


def kernel(**inputs):
    import numpy as _np
    import concourse.bacc as _bacc
    from concourse import mybir as _mybir
    from concourse.bass_utils import run_bass_kernel_spmd as _run

    nc = _bacc.Bacc("TRN2", target_bir_lowering=False, num_devices=1)
    arrays, tensors = {}, {}
    for name in NAMES:
        a = _np.ascontiguousarray(inputs[name])
        arrays[f"in_{name}"] = a
        tensors[name] = nc.dram_tensor(f"in_{name}", a.shape, _mybir.dt.from_np(a.dtype), kind="ExternalInput").ap()
    out = nc.dram_tensor("out_x", (BATCH, SEQ, D), F32, kind="ExternalOutput").ap()
    build(nc, tensors, out)
    r = _run(nc, [arrays], core_ids=[0])
    return r.results[0]["out_x"]
```
